# Optimizing a Trainium2 kernel written in Bass

```python
import numpy as np
import jax
import jax.numpy as jnp

def _softmax(x, axis=-1):
    return jax.nn.softmax(x, axis=axis)

def _gelu(x):
    return jax.nn.gelu(x, approximate=True)

def _silu(x):
    return jax.nn.silu(x)

def _sigmoid(x):
    return jax.nn.sigmoid(x)

def _layernorm(x, axis=-1, eps=1e-05):
    m = jnp.mean(x, axis=axis, keepdims=True)
    v = jnp.var(x, axis=axis, keepdims=True)
    return (x - m) / jnp.sqrt(v + eps)

def _scatter_add(tgt, idx, src, axis=0):
    return tgt.at[idx].add(src)

def _segment_sum(src, seg, n):
    return jax.ops.segment_sum(src, seg, n)
kernel_name = 'mk_recurrent_d1_jaxref_r4_e6d03b'

def setup_inputs(seed: int=0):
    np.random.seed(seed)
    _w = jnp.asarray

    def _L0_attn_setup():
        import jax, jax.numpy as jnp
        import numpy as np
        B, S, D = (8, 512, 256)
        key = jax.random.key(seed)
        k1, k2, k3, k4 = jax.random.split(key, 4)
        x = jax.random.normal(k1, (B, S, D), dtype=jnp.float32)
        W0 = jax.random.normal(k2, (D, D), dtype=jnp.float32) / jnp.sqrt(jnp.float32(D))
        Wkv = jax.random.normal(k3, (2 * D, D), dtype=jnp.float32) / jnp.sqrt(jnp.float32(D))
        bkv = jax.random.normal(k4, (2 * D,), dtype=jnp.float32) * 0.01
        eta = jnp.float32(0.1)
        return {'x': x, 'W0': W0, 'Wkv': Wkv, 'bkv': bkv, 'eta': eta}
    _L0_attn_in = _L0_attn_setup()

    def _L0_ffn_setup():
        import jax, jax.numpy as jnp
        import numpy as np
        HIDDEN = 256
        NUM_EXPERTS = 16
        TOP_K = 6
        EPS = 1e-10
        key = jax.random.key(seed)
        k1, k2, k3, k4 = jax.random.split(key, 4)
        tokens = jax.random.normal(k1, (4, 512, HIDDEN), dtype=jnp.float32)
        bound = 1.0 / np.sqrt(HIDDEN)
        router_w = jax.random.uniform(k2, (NUM_EXPERTS, HIDDEN), jnp.float32, -bound, bound)
        router_b = jax.random.uniform(k3, (NUM_EXPERTS,), jnp.float32, -bound, bound)
        expert_w = jax.random.normal(k4, (NUM_EXPERTS, HIDDEN, HIDDEN), dtype=jnp.float32) / np.sqrt(HIDDEN)
        return {'tokens': tokens, 'router_w': router_w, 'router_b': router_b, 'expert_w': expert_w}
    _L0_ffn_in = _L0_ffn_setup()
    _d = {'L0_attn_x': _L0_attn_in['x'], 'L0_attn_W0': _L0_attn_in['W0'], 'L0_attn_Wkv': _L0_attn_in['Wkv'], 'L0_attn_bkv': _L0_attn_in['bkv'], 'L0_attn_eta': _L0_attn_in['eta'], 'L0_ffn_router_w': _L0_ffn_in['router_w'], 'L0_ffn_router_b': _L0_ffn_in['router_b'], 'L0_ffn_expert_w': _L0_ffn_in['expert_w']}
    _x0 = _d['L0_attn_x']
    _d['L0_attn_x'] = jax.random.normal(jax.random.fold_in(jax.random.key(seed), 1), (8, 1024, 256), dtype=_x0.dtype)
    del _x0
    return _d

def reference(L0_attn_x, L0_attn_W0, L0_attn_Wkv, L0_attn_bkv, L0_attn_eta, L0_ffn_router_w, L0_ffn_router_b, L0_ffn_expert_w):

    def _L0_attn_ref(x, W0, Wkv, bkv, eta):
        import jax, jax.numpy as jnp
        import numpy as np
        B, S, D = (8, 512, 256)
        b, s, d = x.shape
        v = jnp.einsum('bsd,ed->bse', x, Wkv[d:, :]) + bkv[d:]
        scale = 2.0 / (b * d)

        def step(W, inp):
            xt, vt = inp
            y = xt @ W.T
            err = y - vt
            gW = scale * (err.T @ xt)
            return (W - eta * gW, y)
        xs = jnp.swapaxes(x, 0, 1)
        vs = jnp.swapaxes(v, 0, 1)
        _, ys = jax.lax.scan(step, W0, (xs, vs))
        return jnp.swapaxes(ys, 0, 1)

    def _L0_ffn_ref(tokens, router_w, router_b, expert_w):
        import jax, jax.numpy as jnp
        import numpy as np
        HIDDEN = 256
        NUM_EXPERTS = 16
        TOP_K = 6
        EPS = 1e-10
        B, S, H = tokens.shape
        E = expert_w.shape[0]
        T = B * S
        logits = jnp.einsum('bsh,eh->bse', tokens, router_w) + router_b
        probs = jax.nn.softmax(logits, axis=-1)
        top_p, top_i = jax.lax.top_k(probs, TOP_K)
        top_p = top_p / (jnp.sum(top_p, axis=-1, keepdims=True) + EPS)
        x = tokens.reshape(T, H)
        flat_i = top_i.reshape(T, TOP_K)
        flat_p = top_p.reshape(T, TOP_K)
        gate = jnp.zeros((T, E), dtype=flat_p.dtype)
        gate = gate.at[jnp.arange(T)[:, None], flat_i].add(flat_p)
        acc = jnp.maximum(jnp.sum(gate, axis=-1), EPS)
        out = jnp.zeros_like(x)
        for e in range(E):
            out = out + x @ expert_w[e] * gate[:, e:e + 1]
        out = (out / acc[:, None]).reshape(B, S, H)
        out = out + EPS * jnp.sum(top_p, axis=-1, keepdims=True)
        return out
    x = L0_attn_x
    xn = _layernorm(x, axis=-1)
    s = _L0_attn_ref(xn, L0_attn_W0, L0_attn_Wkv, L0_attn_bkv, L0_attn_eta)
    g = _silu(_L0_ffn_ref(xn, L0_ffn_router_w, L0_ffn_router_b, L0_ffn_expert_w))
    x = x + s * g
    return x

_drawn_inputs = setup_inputs


def setup_inputs(seed=0):
    import zlib

    import numpy as np

    out = dict(_drawn_inputs(seed))
    spreads = {}
    factors = {'L0_attn_bkv': 200.0}
    for name, (base, spread) in spreads.items():
        noise = np.random.default_rng([zlib.crc32(name.encode()), seed]).standard_normal(out[name].shape)
        drawn = base * np.exp(spread * noise) if base else spread * noise
        out[name] = jnp.asarray(drawn.astype(out[name].dtype))
    for name, factor in factors.items():
        out[name] = (out[name] * factor).astype(out[name].dtype)
    return out
```

```python
import concourse.bass as bass
from concourse import mybir
from contextlib import ExitStack

FP32 = mybir.dt.float32
FP16 = mybir.dt.float16
INT32 = mybir.dt.int32
ALU = mybir.AluOpType
ACT = mybir.ActivationFunctionType
AX = mybir.AxisListType
ABSMAX = bass.bass_isa.ReduceOp.max

P = 128
BATCH, STEPS, D = 8, 1024, 256
CHUNK_STEPS = P // BATCH
CHUNKS = STEPS // CHUNK_STEPS
HALVES = D // P
EXPERTS, TOP_K = 16, 6
GROUPS = EXPERTS // 2
EXPERT_BANKS = 4
LN_EPS, EPS = 1e-5, 1e-10
VR = D + EXPERTS
X_SCALE = 256.0
W_TOP = 1024.0
W_LOTS = 4
LOT = EXPERTS // W_LOTS
FIRST, LAST = 2, 4
ACT_GROUPS = (1, 5)
DVE_GROUPS = tuple(g for g in range(GROUPS) if g not in ACT_GROUPS)
ZS = 2 * len(DVE_GROUPS)
PS = 2 * len(ACT_GROUPS)
MAGIC = 0x5F3759DF


def program(nc, x_in, w0t_in, wvr_in, expert_in, b_in, rb_in, eta_in, out):
    ctx = ExitStack()
    with ctx:
        def sb(name, shape, dt=FP32):
            return ctx.enter_context(nc.sbuf_tensor(name, shape, dt))

        def pb(name, shape):
            return ctx.enter_context(nc.psum_tensor(name, shape, FP32))

        def sem(name):
            return ctx.enter_context(nc.semaphore(name))

        x_all = sb("x_all", [P, CHUNKS, D])
        w_raw = sb("w_raw", [P, HALVES, EXPERTS, D])
        w_hi = sb("w_hi", [P, HALVES, EXPERTS, D], FP16)
        w_lo = sb("w_lo", [P, HALVES, EXPERTS, D], FP16)
        vr_raw = sb("vr_raw", [P, HALVES, VR])
        vr_hi = sb("vr_hi", [P, HALVES, VR], FP16)
        vr_lo = sb("vr_lo", [P, HALVES, VR], FP16)
        state = sb("state", [P, HALVES, D])
        b_row = sb("b_row", [P, D])
        rb_row = sb("rb_row", [P, EXPERTS])
        eta = sb("eta", [P, 1])
        neg_c = sb("neg_c", [P, 1])
        ident = sb("ident", [P, P])
        ones = sb("ones", [P, 1])
        lower = sb("lower", [P, P])
        upper = sb("upper", [P, P])
        absmax = sb("absmax", [P, 2 + W_LOTS])
        allmax = sb("allmax", [P, 2 + W_LOTS])
        power = sb("power", [P, 2 + W_LOTS])
        rpower = sb("rpower", [P, 2 + W_LOTS])
        scale = sb("scale", [P, 2 + W_LOTS])
        unscale = sb("unscale", [P, 2 + W_LOTS])
        un_e = sb("un_e", [P, EXPERTS])
        q = sb("q", [P, 1])
        half_unq = sb("half_unq", [P, 1])

        stats = sb("stats", [P, 2, 6])
        mv = sb("mv", [P, 2, 2])
        vare = sb("vare", [P, 2, 1])
        nvh = sb("nvh", [P, 2, 1])
        half_bits = sb("half_bits", [P, 2, 1], INT32)
        rs = [sb(f"rs{n}", [P, 2, 1]) for n in range(4)]
        nt_a = sb("nt_a", [P, 2, 3])
        nt_b = sb("nt_b", [P, 2, 3])
        nt_c = sb("nt_c", [P, 2, 3])
        neg_half = sb("neg_half", [P, 1])
        three_halves = sb("three_halves", [P, 1])
        xn = sb("xn", [P, 2, D])
        xt = sb("xt", [P, HALVES, P])
        xt_hi = sb("xt_hi", [P, 2, HALVES, P], FP16)
        xt_lo = sb("xt_lo", [P, 2, HALVES, P], FP16)
        n1 = sb("n1", [P, P])
        n1t = sb("n1t", [P, P])
        n2 = sb("n2", [P, P])
        n2t = sb("n2t", [P, P])
        n4 = sb("n4", [P, P])
        n4t = sb("n4t", [P, P])
        s3 = sb("s3", [P, P])
        s2 = sb("s2", [P, P])
        s1 = sb("s1", [P, P])
        s0 = sb("s0", [P, P])
        txt = sb("txt", [P, HALVES, P])
        neg_t1 = sb("neg_t1", [P, 1])
        err = sb("err", [P, 2, D])
        v = sb("v", [P, 2, D])
        y = sb("y", [P, 2, D])
        logit = sb("logit", [P, 2, EXPERTS])
        top_l = sb("top_l", [P, 2, 8])
        neg_max = sb("neg_max", [P, 2, 1])
        ex = sb("ex", [P, 2, EXPERTS + 2])
        ex_sum = sb("ex_sum", [P, 2, 1])
        top_e = sb("top_e", [P, 2, 8])
        rest = sb("rest", [P, 2, EXPERTS + 2])
        ex_eps = sb("ex_eps", [P, 2, 1])
        sel = sb("sel", [P, 2, EXPERTS])
        sel_sum = sb("sel_sum", [P, 2, 1])
        denom = sb("denom", [P, 2, 1])
        rdenom = sb("rdenom", [P, 2, 1])
        eps_term = sb("eps_term", [P, 2, 1])
        acc = sb("acc", [P, 2, 1])
        racc = sb("racc", [P, 2, 1])
        factor = sb("factor", [P, 2, 1])
        gate = sb("gate", [P, 2, EXPERTS])
        zacc = sb("zacc", [P, 2, 2, D])
        part = sb("part", [P, 2, PS, D])
        psum01 = sb("psum01", [P, D])
        psum23 = sb("psum23", [P, D])
        parts = sb("parts", [P, D])
        zeo = sb("zeo", [P, D])
        z = sb("z", [P, 2, D])
        th = sb("th", [P, 2, D])
        zt = sb("zt", [P, D])
        silu2 = sb("silu2", [P, 2, D])
        sg = sb("sg", [P, 2, D])

        t_bank = pb("t_bank", [P, HALVES, D])
        vr_bank = pb("vr_bank", [P, 512])
        inv_bank = pb("inv_bank", [P, 4, P])
        mem_bank = pb("mem_bank", [P, 512])
        e_bank = [pb(f"e_bank{n}", [P, 512]) for n in range(EXPERT_BANKS)]

        x_loaded = sem("x_loaded")
        small_loaded = sem("small_loaded")
        vr_loaded = sem("vr_loaded")
        w_loaded = [sem(f"w_loaded{n}") for n in range(W_LOTS)]
        stored = sem("stored")
        const_ready = sem("const_ready")
        mask_scaled = sem("mask_scaled")
        max_ready = sem("max_ready")
        allmax_ready = sem("allmax_ready")
        scale_ready = sem("scale_ready")
        hi_ready = sem("hi_ready")
        lo_ready = sem("lo_ready")
        setup_step = sem("setup_step")
        setup_pool = sem("setup_pool")
        state_ready = sem("state_ready")
        stat_step = sem("stat_step")
        newton = sem("newton")
        xn_ready = sem("xn_ready")
        transposed = sem("transposed")
        xh_ready = sem("xh_ready")
        xt_ready = sem("xt_ready")
        xl_ready = sem("xl_ready")
        vr_done = sem("vr_done")
        v_ready = sem("v_ready")
        route = sem("route")
        ex_ready = sem("ex_ready")
        gram_done = sem("gram_done")
        n1_ready = sem("n1_ready")
        p2_done = sem("p2_done")
        n2_ready = sem("n2_ready")
        p4_done = sem("p4_done")
        n4_ready = sem("n4_ready")
        p8_done = sem("p8_done")
        s3_ready = sem("s3_ready")
        s2_done = sem("s2_done")
        s2_ready = sem("s2_ready")
        s1_done = sem("s1_done")
        s1_ready = sem("s1_ready")
        s0_done = sem("s0_done")
        s0_ready = sem("s0_ready")
        tx_done = sem("tx_done")
        tx_ready = sem("tx_ready")
        err_done = sem("err_done")
        err_ready = sem("err_ready")
        grad_done = sem("grad_done")
        group_done = [sem(f"group_done{n}") for n in range(EXPERT_BANKS)]
        z_step = sem("z_step")
        part_step = sem("part_step")
        part_sum = sem("part_sum")
        z_sum = sem("z_sum")
        y_ready = sem("y_ready")
        th_ready = sem("th_ready")
        zt_ready = sem("zt_ready")
        silu_ready = sem("silu_ready")
        sg_ready = sem("sg_ready")
        out_ready = sem("out_ready")
        ROUTE, STAT, NEWTON = 15, 5, 13

        def past(k, n):
            return not isinstance(k, int) or k >= n

        def in_loop(eng, body):
            for k in range(FIRST):
                body(k, k % 2)
            with eng.Fori(0, (CHUNKS - FIRST - LAST) // 2) as pair:
                for r in range(2):
                    body(2 * pair + (FIRST + r), r)
            for k in range(CHUNKS - LAST, CHUNKS):
                body(k, k % 2)

        def exists(k):
            return not isinstance(k, int) or k < CHUNKS

        block = ctx.enter_context(nc.Block())

        @block.sync
        def _(sp):
            sp.dma_start(x_all[:, 0, :], x_in[:, 0, :]).then_inc(x_loaded, 16)
            with sp.Fori(1, CHUNKS) as k:
                sp.wait_ge(x_loaded, 16 * k)
                sp.dma_start(x_all[:, k, :], x_in[:, k, :]).then_inc(x_loaded, 16)
            with sp.Fori(0, CHUNKS) as k:
                sp.wait_ge(out_ready, k + 1)
                sp.dma_start(out[:, k, :], x_all[:, k, :]).then_inc(stored, 16)
            sp.wait_ge(stored, 16 * CHUNKS)

        @block.gpsimd
        def _(pool):
            nc.gpsimd.memset(ident[:], 0.0).then_inc(setup_pool, 1)
            nc.gpsimd.memset(lower[:], 1.0).then_inc(setup_pool, 1)
            nc.gpsimd.memset(upper[:], 1.0).then_inc(setup_pool, 1)
            pool.wait_ge(setup_pool, 3)
            nc.gpsimd.affine_select(out=ident[:], in_=ident[:], compare_op=ALU.not_equal, fill=1.0, base=0,
                                    pattern=[[-1, P]], channel_multiplier=1).then_inc(const_ready, 1)
            low3 = lower[:].rearrange("p (j r) -> p j r", r=BATCH)
            upp3 = upper[:].rearrange("p (j r) -> p j r", r=BATCH)
            nc.gpsimd.affine_select(out=low3, in_=low3, compare_op=ALU.is_ge, fill=0.0, base=-BATCH,
                                    pattern=[[-BATCH, CHUNK_STEPS], [0, BATCH]],
                                    channel_multiplier=1).then_inc(const_ready, 1)
            nc.gpsimd.affine_select(out=upp3, in_=upp3, compare_op=ALU.is_ge, fill=0.0, base=-1,
                                    pattern=[[BATCH, CHUNK_STEPS], [0, BATCH]],
                                    channel_multiplier=-1).then_inc(const_ready, 1)
            nc.gpsimd.memset(ones[:], 1.0).then_inc(const_ready, 1)
            nc.gpsimd.memset(neg_half[:], -0.5).then_inc(const_ready, 1)
            nc.gpsimd.memset(three_halves[:], 1.5).then_inc(const_ready, 1)
            nc.gpsimd.memset(ex[:], -1.0).then_inc(const_ready, 1)
            for t in (n2, n2t, n4, n4t):
                nc.gpsimd.memset(t[:], 0.0).then_inc(const_ready, 1)
            pool.wait_ge(const_ready, 1)
            for t in (s3, s2, s1, s0):
                nc.gpsimd.tensor_copy(t[:], ident[:]).then_inc(const_ready, 1)

            def newton_steps(k, r):
                pool.wait_ge(stat_step, STAT * (k + 1))
                base = NEWTON * k
                nc.gpsimd.tensor_tensor(nvh[:, r, :], vare[:, r, :], neg_half[:], ALU.mult).then_inc(newton, 1)
                for n in range(3):
                    guess, a, b, c = rs[n][:, r, :], nt_a[:, r, n:n + 1], nt_b[:, r, n:n + 1], nt_c[:, r, n:n + 1]
                    nc.gpsimd.tensor_tensor(a, guess, guess, ALU.mult).then_inc(newton, 1)
                    pool.wait_ge(newton, base + (4 * n + 2))
                    nc.gpsimd.tensor_tensor(b, a, nvh[:, r, :], ALU.mult).then_inc(newton, 1)
                    pool.wait_ge(newton, base + (4 * n + 3))
                    nc.gpsimd.tensor_tensor(c, b, three_halves[:], ALU.add).then_inc(newton, 1)
                    pool.wait_ge(newton, base + (4 * n + 4))
                    if n == 2 and past(k, 2):
                        pool.wait_ge(xn_ready, k - 1)
                    nc.gpsimd.tensor_tensor(rs[n + 1][:, r, :], guess, c, ALU.mult).then_inc(newton, 1)
                    if n < 2:
                        pool.wait_ge(newton, base + (4 * n + 5))

            pool.wait_ge(const_ready, 7)
            newton_steps(0, 0)
            newton_steps(1, 1)
            for n in range(2 + W_LOTS):
                pool.wait_ge(max_ready, n + 1)
                nc.gpsimd.partition_all_reduce(allmax[:, n:n + 1], absmax[:, n:n + 1], P,
                                               ABSMAX).then_inc(allmax_ready, 1)
            newton_steps(2, 0)

            def z_total(k, r):
                pool.wait_ge(z_step, ZS * (k + 1))
                nc.gpsimd.tensor_tensor(zeo[:], zacc[:, r, 0, :], zacc[:, r, 1, :], ALU.add).then_inc(z_sum, 1)
                pool.wait_ge(part_sum, 3 * (k + 1))
                pool.wait_ge(z_sum, 2 * k + 1)
                if past(k, 2):
                    pool.wait_ge(th_ready, k - 1)
                nc.gpsimd.tensor_tensor(z[:, r, :], zeo[:], parts[:], ALU.add).then_inc(z_sum, 1)

            def silu_of(k, r):
                pool.wait_ge(th_ready, k + 1)
                nc.gpsimd.tensor_tensor(zt[:], z[:, r, :], th[:, r, :], ALU.mult).then_inc(zt_ready, 1)
                pool.wait_ge(zt_ready, k + 1)
                if past(k, 2):
                    pool.wait_ge(sg_ready, k - 1)
                nc.gpsimd.tensor_tensor(silu2[:, r, :], z[:, r, :], zt[:], ALU.add).then_inc(silu_ready, 1)

            def result(k, r):
                pool.wait_ge(sg_ready, k + 1)
                nc.gpsimd.tensor_tensor(x_all[:, k, :], sg[:, r, :], x_all[:, k, :],
                                        ALU.add).then_inc(out_ready, 1)

            def body(k, r):
                if past(k, 1):
                    z_total(k - 1, 1 - r)
                pool.wait_ge(err_ready, k + 1)
                pool.wait_ge(v_ready, k + 1)
                if past(k, 2):
                    pool.wait_ge(sg_ready, k - 1)
                nc.gpsimd.tensor_tensor(y[:, r, :], err[:, r, :], v[:, r, :], ALU.add).then_inc(y_ready, 1)
                if past(k, 1):
                    silu_of(k - 1, 1 - r)
                pool.wait_ge(part_step, PS * k + 2)
                if past(k, 1):
                    pool.wait_ge(part_sum, 3 * k)
                nc.gpsimd.tensor_tensor(psum01[:], part[:, r, 0, :], part[:, r, 1, :],
                                        ALU.add).then_inc(part_sum, 1)
                if past(k, 1):
                    result(k - 1, 1 - r)
                if exists(k + 3):
                    newton_steps(k + 3, 1 - r)
                pool.wait_ge(part_step, PS * k + 4)
                nc.gpsimd.tensor_tensor(psum23[:], part[:, r, 2, :], part[:, r, 3, :],
                                        ALU.add).then_inc(part_sum, 1)
                pool.wait_ge(part_sum, 3 * k + 2)
                if past(k, 1):
                    pool.wait_ge(z_sum, 2 * k)
                nc.gpsimd.tensor_tensor(parts[:], psum01[:], psum23[:], ALU.add).then_inc(part_sum, 1)

            in_loop(pool, body)
            last = CHUNKS - 1
            z_total(last, last % 2)
            silu_of(last, last % 2)
            result(last, last % 2)

        @block.scalar
        def _(act):
            act.dma_start(vr_raw[:], wvr_in).then_inc(vr_loaded, 16)
            act.dma_start(state[:], w0t_in).then_inc(small_loaded, 16)
            act.dma_start(b_row[:], b_in.broadcast_to([P, D])).then_inc(small_loaded, 16)
            act.dma_start(rb_row[:], rb_in.broadcast_to([P, EXPERTS])).then_inc(small_loaded, 16)
            act.dma_start(eta[:], eta_in.broadcast_to([P, 1])).then_inc(small_loaded, 16)
            for n in range(W_LOTS):
                act.dma_start(w_raw[:, :, n * LOT:(n + 1) * LOT, :],
                              expert_in[:, :, n * LOT:(n + 1) * LOT, :]).then_inc(w_loaded[n], 16)

            def transposed_parts(k, r):
                act.wait_ge(transposed, k + 1)
                if past(k, 2):
                    act.wait_ge(group_done[EXPERT_BANKS - 1], 2 * (k - 1))
                nc.scalar.activation(xt_hi[:, r, :, :], t_bank[:, :, 0:P], ACT.Copy,
                                     scale=X_SCALE).then_inc(xh_ready, 1)
                if past(k, 1):
                    act.wait_ge(gram_done, k)
                nc.scalar.activation(xt[:], t_bank[:, :, 0:P], ACT.Copy).then_inc(xt_ready, 1)

            def tx_out(k, r):
                act.wait_ge(tx_done, k + 1)
                if past(k, 1):
                    act.wait_ge(err_ready, k)
                nc.scalar.activation(txt[:], mem_bank[:, 0:D].rearrange("p (h t) -> p h t", h=HALVES), ACT.Copy)
                nc.scalar.activation(neg_t1[:], mem_bank[:, D:D + 1], ACT.Copy, scale=-1.0).then_inc(tx_ready, 1)

            def group(k, r, n):
                g = ACT_GROUPS[n]
                bank = g % EXPERT_BANKS
                act.wait_ge(group_done[bank], 2 * k + (g // EXPERT_BANKS + 1))
                if n == 0:
                    act.wait_ge(route, ROUTE * (k + 1))
                    if past(k, 2):
                        act.wait_ge(part_sum, 3 * (k - 1))
                for j in range(2):
                    e = 2 * g + j
                    nc.scalar.activation(part[:, r, 2 * n + j, :], e_bank[bank][:, j * D:(j + 1) * D], ACT.Copy,
                                         scale=gate[:, r, e:e + 1]).then_inc(part_step, 1)

            def squares(k):
                act.wait_ge(p2_done, k + 1)
                nc.scalar.activation(n2[:, 0:P - 16], inv_bank[:, 0, 0:P - 16], ACT.Copy)
                nc.scalar.activation(n2t[:, 16:P], inv_bank[:, 1, 16:P], ACT.Copy).then_inc(n2_ready, 1)

            def fourths(k):
                act.wait_ge(p4_done, k + 1)
                nc.scalar.activation(n4[:, 0:P - 32], inv_bank[:, 0, 0:P - 32], ACT.Copy)
                nc.scalar.activation(n4t[:, 64:P], inv_bank[:, 1, 64:P], ACT.Copy).then_inc(n4_ready, 1)

            def exponent(k, r):
                act.wait_ge(route, ROUTE * k + 3)
                nc.scalar.activation(ex[:, r, 0:EXPERTS], logit[:, r, :], ACT.Exp, bias=neg_max[:, r, :],
                                     accum_out=ex_sum[:, r, :]).then_inc(ex_ready, 1)

            def tanh_of(k, r):
                act.wait_ge(z_sum, 2 * (k + 1))
                if past(k, 2):
                    act.wait_ge(silu_ready, k - 1)
                nc.scalar.activation(th[:, r, :], z[:, r, :], ACT.Tanh, scale=0.5).then_inc(th_ready, 1)

            act.wait_ge(vr_loaded, 16)
            act.wait_ge(scale_ready, 2)
            nc.scalar.activation(vr_hi[:, :, 0:D], vr_raw[:, :, 0:D], ACT.Copy, scale=scale[:, 0:1]).then_inc(hi_ready, 1)
            nc.scalar.activation(vr_hi[:, :, D:VR], vr_raw[:, :, D:VR], ACT.Copy,
                                 scale=scale[:, 1:2]).then_inc(hi_ready, 1)
            act.wait_ge(const_ready, 15)
            transposed_parts(0, 0)
            squares(0)
            exponent(0, 0)
            fourths(0)
            for n in range(W_LOTS):
                act.wait_ge(scale_ready, 3 + n)
                act.wait_ge(w_loaded[n], 16)
                lot = slice(n * LOT, (n + 1) * LOT)
                for h in range(HALVES):
                    last = nc.scalar.activation(w_hi[:, h, lot, :], w_raw[:, h, lot, :], ACT.Copy,
                                                scale=scale[:, 2 + n:3 + n])
                last.then_inc(hi_ready, 1)

            def body(k, r):
                if exists(k + 1):
                    transposed_parts(k + 1, 1 - r)
                tx_out(k, r)
                if past(k, 1):
                    tanh_of(k - 1, 1 - r)
                group(k, r, 0)
                if exists(k + 1):
                    squares(k + 1)
                    exponent(k + 1, 1 - r)
                    fourths(k + 1)
                group(k, r, 1)

            in_loop(act, body)
            last = CHUNKS - 1
            tanh_of(last, last % 2)

        @block.vector
        def _(dve):
            def stats_waits(k):
                dve.wait_ge(x_loaded, 16 * (k + 1))

            def stats_first(k, r):
                nc.vector.bn_stats(stats[:, r, :], x_all[:, k, :]).then_inc(stat_step, 1)

            def stats_second_waits(k):
                if past(k, 2):
                    dve.wait_ge(xn_ready, k - 1)
                dve.wait_ge(stat_step, STAT * k + 1)

            def stats_second(k, r):
                nc.vector.bn_aggr(mv[:, r, :], stats[:, r, :]).then_inc(stat_step, 1)

            def guess_of(k, r):
                base = STAT * k
                dve.wait_ge(stat_step, base + 2)
                nc.vector.tensor_scalar(vare[:, r, :], mv[:, r, 1:2], LN_EPS, None, ALU.add).then_inc(stat_step, 1)
                dve.wait_ge(stat_step, base + 3)
                nc.vector.tensor_scalar(half_bits[:, r, :], vare[:, r, :].bitcast(INT32), 1, None,
                                        ALU.logical_shift_right).then_inc(stat_step, 1)
                dve.wait_ge(stat_step, base + 4)
                nc.vector.tensor_scalar(rs[0][:, r, :].bitcast(INT32), half_bits[:, r, :], -1.0, float(MAGIC),
                                        ALU.mult, ALU.add).then_inc(stat_step, 1)

            def stats_of(k, r):
                stats_waits(k)
                stats_first(k, r)
                stats_second_waits(k)
                stats_second(k, r)
                guess_of(k, r)

            def normalize(k, r):
                dve.wait_ge(newton, NEWTON * (k + 1))
                if past(k, 2):
                    dve.wait_ge(grad_done, k - 1)
                nc.vector.tensor_scalar(xn[:, r, :], x_all[:, k, :], mv[:, r, 0:1], rs[3][:, r, :],
                                        ALU.subtract, ALU.mult).then_inc(xn_ready, 1)

            def largest(n, src):
                nc.vector.tensor_reduce(absmax[:, n:n + 1], src, AX.XY if len(src.shape) == 3 else AX.XYZ, ALU.max,
                                        apply_absolute_value=True).then_inc(max_ready, 1)

            steps = [0]

            def link(ins):
                steps[0] += 1
                ins.then_inc(setup_step, 1)
                dve.wait_ge(setup_step, steps[0])

            def scale_of(n):
                dve.wait_ge(allmax_ready, n + 1)
                c = slice(n, n + 1)
                link(nc.vector.tensor_scalar(power[:, c], allmax[:, c], 2.0 ** -20, None, ALU.max))
                link(nc.vector.tensor_scalar(power[:, c].bitcast(INT32), power[:, c].bitcast(INT32), 0x7F800000, None,
                                             ALU.bitwise_and))
                link(nc.vector.reciprocal(rpower[:, c], power[:, c]))
                nc.vector.tensor_scalar(unscale[:, c], power[:, c], 1.0 / (W_TOP * X_SCALE), None, ALU.mult)
                link(nc.vector.tensor_scalar(scale[:, c], rpower[:, c], W_TOP, None, ALU.mult))
                nc.vector.tensor_copy(scale[:, c], scale[:, c]).then_inc(scale_ready, 1)

            def low_parts(k, r):
                dve.wait_ge(xh_ready, k + 1)
                if past(k, 1):
                    dve.wait_ge(group_done[EXPERT_BANKS - 1], 2 * (k - 1)) if past(k, 2) else None
                dve.wait_ge(xt_ready, k + 1)
                nc.vector.scalar_tensor_tensor(out=xt_lo[:, r, :, :], in0=t_bank[:, :, 0:P], scalar=X_SCALE,
                                               in1=xt_hi[:, r, :, :], op0=ALU.mult,
                                               op1=ALU.subtract).then_inc(xl_ready, 1)

            def gram_out(k):
                dve.wait_ge(gram_done, k + 1)
                nc.vector.tensor_tensor(n1[:], inv_bank[:, 0, :], lower[:], ALU.mult)
                nc.vector.tensor_tensor(n1t[:], inv_bank[:, 0, :], upper[:], ALU.mult).then_inc(n1_ready, 1)

            def logits_out(k, r):
                dve.wait_ge(vr_done, k + 1)
                base = ROUTE * k
                nc.vector.scalar_tensor_tensor(out=logit[:, r, :], in0=vr_bank[:, D:VR], scalar=unscale[:, 1:2],
                                               in1=rb_row[:], op0=ALU.mult, op1=ALU.add).then_inc(route, 1)
                if past(k, 2):
                    dve.wait_ge(y_ready, k - 1)
                nc.vector.tensor_tensor(v[:, r, :], vr_bank[:, 0:D], b_row[:], ALU.add).then_inc(v_ready, 1)

            def top_logit_waits(k):
                dve.wait_ge(route, ROUTE * k + 1)

            def top_logit(k, r):
                base = ROUTE * k
                nc.vector.max(top_l[:, r, :], logit[:, r, :]).then_inc(route, 1)
                dve.wait_ge(route, base + 2)
                nc.vector.tensor_scalar(neg_max[:, r, :], top_l[:, r, 0:1], -1.0, None, ALU.mult).then_inc(route, 1)

            def top_gates(k, r):
                base = ROUTE * k
                nc.vector.max(top_e[:, r, :], ex[:, r, 0:EXPERTS]).then_inc(route, 1)
                dve.wait_ge(route, base + 4)
                nc.vector.memset(top_e[:, r, TOP_K:8], -1.0).then_inc(route, 1)
                dve.wait_ge(route, base + 5)
                nc.vector.tensor_scalar(ex_eps[:, r, :], ex_sum[:, r, :], EPS, None, ALU.mult).then_inc(route, 1)
                nc.vector.match_replace(rest[:, r, :], top_e[:, r, :], ex[:, r, :], 0.0).then_inc(route, 1)
                dve.wait_ge(route, base + 7)
                nc.vector.scalar_tensor_tensor(out=sel[:, r, :], in0=ex[:, r, 0:EXPERTS], scalar=1.0,
                                               in1=rest[:, r, 0:EXPERTS], op0=ALU.mult, op1=ALU.subtract,
                                               accum_out=sel_sum[:, r, :]).then_inc(route, 1)

            def gates_norm(k, r):
                base = ROUTE * k
                dve.wait_ge(route, base + 8)
                nc.vector.tensor_tensor(denom[:, r, :], ex_eps[:, r, :], sel_sum[:, r, :], ALU.add).then_inc(route, 1)
                dve.wait_ge(route, base + 9)
                nc.vector.reciprocal(rdenom[:, r, :], denom[:, r, :]).then_inc(route, 1)
                dve.wait_ge(route, base + 10)
                nc.vector.tensor_scalar(acc[:, r, :], sel_sum[:, r, :], rdenom[:, r, :], EPS, ALU.mult,
                                        ALU.max).then_inc(route, 1)
                nc.vector.tensor_scalar(eps_term[:, r, :], sel_sum[:, r, :], rdenom[:, r, :], EPS, ALU.mult,
                                        ALU.mult).then_inc(route, 1)

            def gates_scaled(k, r):
                base = ROUTE * k
                dve.wait_ge(route, base + 11)
                nc.vector.reciprocal(racc[:, r, :], acc[:, r, :]).then_inc(route, 1)
                dve.wait_ge(route, base + 13)
                nc.vector.tensor_tensor(factor[:, r, :], rdenom[:, r, :], racc[:, r, :], ALU.mult).then_inc(route, 1)
                dve.wait_ge(route, base + 14)
                if past(k, 2):
                    dve.wait_ge(part_step, PS * (k - 1))
                nc.vector.scalar_tensor_tensor(out=gate[:, r, :], in0=sel[:, r, :], scalar=factor[:, r, :],
                                               in1=un_e[:], op0=ALU.mult, op1=ALU.mult).then_inc(route, 1)

            def identity_plus_eighth(k):
                dve.wait_ge(p8_done, k + 1)
                nc.vector.tensor_tensor(s3[:, 64:P], inv_bank[:, 0, 64:P], ident[:, 64:P], ALU.add).then_inc(s3_ready, 1)

            def add_product(k, done, dst, src, first, op, ready):
                dve.wait_ge(done, k + 1)
                nc.vector.tensor_tensor(dst[:, first:P], src[:, first:P], inv_bank[:, 0, first:P], op).then_inc(ready, 1)

            def err_out(k, r):
                dve.wait_ge(err_done, k + 1)
                dve.wait_ge(tx_ready, k + 1)
                if past(k, 2):
                    dve.wait_ge(y_ready, k - 1)
                nc.vector.scalar_tensor_tensor(out=err[:, r, :], in0=b_row[:], scalar=neg_t1[:], in1=mem_bank[:, 0:D],
                                               op0=ALU.mult, op1=ALU.add).then_inc(err_ready, 1)

            def update(k):
                dve.wait_ge(grad_done, k + 1)
                flat = state[:].rearrange("p h e -> p (h e)")
                nc.vector.scalar_tensor_tensor(out=flat, in0=mem_bank[:], scalar=neg_c[:], in1=flat,
                                               op0=ALU.mult, op1=ALU.add).then_inc(state_ready, 1)

            def group(k, r, n):
                g = DVE_GROUPS[n]
                bank = g % EXPERT_BANKS
                base = ZS * k
                dve.wait_ge(group_done[bank], 2 * k + (g // EXPERT_BANKS + 1))
                if n == 0:
                    dve.wait_ge(route, ROUTE * (k + 1))
                    if past(k, 2):
                        dve.wait_ge(z_sum, 2 * (k - 1))
                for j in range(2):
                    e = 2 * g + j
                    src = e_bank[bank][:, j * D:(j + 1) * D]
                    if n == 0:
                        nc.vector.tensor_scalar(zacc[:, r, j, :], src, gate[:, r, e:e + 1],
                                                None if j else eps_term[:, r, :], ALU.mult,
                                                ALU.bypass if j else ALU.add).then_inc(z_step, 1)
                    else:
                        dve.wait_ge(z_step, base + (2 * n + j - 1))
                        nc.vector.scalar_tensor_tensor(out=zacc[:, r, j, :], in0=src, scalar=gate[:, r, e:e + 1],
                                                       in1=zacc[:, r, j, :], op0=ALU.mult,
                                                       op1=ALU.add).then_inc(z_step, 1)

            def gated(k, r):
                dve.wait_ge(silu_ready, k + 1)
                dve.wait_ge(y_ready, k + 1)
                if past(k, 2):
                    dve.wait_ge(out_ready, k - 1)
                nc.vector.scalar_tensor_tensor(out=sg[:, r, :], in0=silu2[:, r, :], scalar=half_unq[:],
                                               in1=y[:, r, :], op0=ALU.mult, op1=ALU.mult).then_inc(sg_ready, 1)

            for k in range(2):
                stats_of(k, k)
            for k in range(2):
                normalize(k, k)
            dve.wait_ge(vr_loaded, 16)
            largest(0, vr_raw[:, :, 0:D])
            largest(1, vr_raw[:, :, D:VR])
            dve.wait_ge(small_loaded, 64)
            link(nc.vector.tensor_scalar(neg_c[:], eta[:], -2.0 / (BATCH * D), None, ALU.mult))
            dve.wait_ge(const_ready, 3)
            c_pos = power[:, 2:3]
            link(nc.vector.tensor_scalar(c_pos, neg_c[:], -1.0, None, ALU.mult))
            nc.vector.tensor_scalar(lower[:], lower[:], c_pos, None, ALU.mult).then_inc(mask_scaled, 1)
            nc.vector.tensor_scalar(upper[:], upper[:], c_pos, None, ALU.mult).then_inc(mask_scaled, 1)
            link(nc.vector.tensor_tensor(state[:], state[:], vr_raw[:, :, 0:D], ALU.subtract))
            scale_of(0)
            scale_of(1)
            for n, c in ((0, slice(0, D)), (1, slice(D, VR))):
                dve.wait_ge(hi_ready, n + 1)
                nc.vector.scalar_tensor_tensor(out=vr_lo[:, :, c], in0=vr_raw[:, :, c], scalar=scale[:, n:n + 1],
                                               in1=vr_hi[:, :, c], op0=ALU.mult, op1=ALU.subtract).then_inc(lo_ready, 1)
            link(nc.vector.tensor_scalar(q[:], scale[:, 0:1], X_SCALE, None, ALU.mult))
            nc.vector.tensor_scalar(half_unq[:], unscale[:, 0:1], 0.5, None, ALU.mult)
            nc.vector.tensor_scalar(b_row[:], b_row[:], q[:], None, ALU.mult).then_inc(setup_step, 1)
            steps[0] += 1
            nc.vector.tensor_scalar(state[:], state[:], q[:], None, ALU.mult).then_inc(state_ready, 1)
            dve.wait_ge(setup_step, steps[0])

            dve.wait_ge(mask_scaled, 2)
            dve.wait_ge(const_ready, 15)
            low_parts(0, 0)
            logits_out(0, 0)
            top_logit_waits(0)
            gram_out(0)
            top_logit(0, 0)
            dve.wait_ge(w_loaded[0], 16)
            largest(2, w_raw[:, :, 0:LOT, :])
            identity_plus_eighth(0)
            add_product(0, s2_done, s2, s3, 32, ALU.add, s2_ready)
            add_product(0, s1_done, s1, s2, 16, ALU.add, s1_ready)
            add_product(0, s0_done, s0, s1, 8, ALU.subtract, s0_ready)
            stats_of(2, 0)
            for n in range(W_LOTS):
                lot = slice(n * LOT, (n + 1) * LOT)
                scale_of(2 + n)
                if n + 1 < W_LOTS:
                    dve.wait_ge(w_loaded[n + 1], 16)
                    largest(3 + n, w_raw[:, :, (n + 1) * LOT:(n + 2) * LOT, :])
                for e in range(n * LOT, (n + 1) * LOT):
                    nc.vector.tensor_copy(un_e[:, e:e + 1], unscale[:, 2 + n:3 + n])
                dve.wait_ge(hi_ready, 3 + n)
                for h in range(HALVES):
                    dst = nc.vector.scalar_tensor_tensor(
                        out=w_lo[:, h, lot, :].rearrange("p e d -> p (e d)"),
                        in0=w_raw[:, h, lot, :].rearrange("p e d -> p (e d)"), scalar=scale[:, 2 + n:3 + n],
                        in1=w_hi[:, h, lot, :].rearrange("p e d -> p (e d)"), op0=ALU.mult, op1=ALU.subtract)
                dst.then_inc(lo_ready, 1)
            dve.wait_ge(ex_ready, 1)
            top_gates(0, 0)
            gates_norm(0, 0)
            gates_scaled(0, 0)

            def body(k, r):
                nxt, nn, nnn = exists(k + 1), exists(k + 2), exists(k + 3)
                if nxt:
                    low_parts(k + 1, 1 - r)
                group(k, r, 0)
                if nnn:
                    stats_waits(k + 3)
                err_out(k, r)
                if nnn:
                    stats_first(k + 3, 1 - r)
                if nxt:
                    logits_out(k + 1, 1 - r)
                    top_logit_waits(k + 1)
                if nnn:
                    stats_second_waits(k + 3)
                if nxt:
                    gram_out(k + 1)
                    top_logit(k + 1, 1 - r)
                if nnn:
                    stats_second(k + 3, 1 - r)
                if past(k, 1):
                    gated(k - 1, 1 - r)
                if nnn:
                    guess_of(k + 3, 1 - r)
                update(k)
                if nxt:
                    dve.wait_ge(ex_ready, k + 2)
                if nn:
                    normalize(k + 2, r)
                if nxt:
                    top_gates(k + 1, 1 - r)
                group(k, r, 1)
                if nxt:
                    gates_norm(k + 1, 1 - r)
                group(k, r, 2)
                if nxt:
                    identity_plus_eighth(k + 1)
                group(k, r, 3)
                if nxt:
                    add_product(k + 1, s2_done, s2, s3, 32, ALU.add, s2_ready)
                    gates_scaled(k + 1, 1 - r)
                    add_product(k + 1, s1_done, s1, s2, 16, ALU.add, s1_ready)
                group(k, r, 4)
                if nxt:
                    add_product(k + 1, s0_done, s0, s1, 8, ALU.subtract, s0_ready)
                group(k, r, 5)

            in_loop(dve, body)
            last = CHUNKS - 1
            gated(last, last % 2)

        @block.tensor
        def _(pe):
            def transposes(k, r):
                pe.wait_ge(xn_ready, k + 1)
                if past(k, 1):
                    pe.wait_ge(xl_ready, k)
                for h in range(HALVES):
                    last = nc.tensor.transpose(t_bank[:, h, 0:P], xn[:, r, h * P:(h + 1) * P], ident[:])
                last.then_inc(transposed, 1)

            def split_product(dst, r, hi, lo):
                for h in range(HALVES):
                    nc.tensor.matmul(dst, xt_hi[:, r, h, :], hi(h), start=(h == 0), stop=False)
                    nc.tensor.matmul(dst, xt_hi[:, r, h, :], lo(h), start=False, stop=False)
                for h in range(HALVES):
                    last = nc.tensor.matmul(dst, xt_lo[:, r, h, :], hi(h), start=False, stop=(h == HALVES - 1))
                return last

            def values_and_logits(k, r):
                pe.wait_ge(xh_ready, k + 1)
                pe.wait_ge(xl_ready, k + 1)
                if past(k, 1):
                    pe.wait_ge(v_ready, k)
                split_product(vr_bank[:, 0:VR], r, lambda h: vr_hi[:, h, :], lambda h: vr_lo[:, h, :]).then_inc(vr_done, 1)

            def gram(k):
                pe.wait_ge(xt_ready, k + 1)
                for h in range(HALVES):
                    last = nc.tensor.matmul(inv_bank[:, 0, :], xt[:, h, :], xt[:, h, :], start=(h == 0),
                                            stop=(h == HALVES - 1))
                last.then_inc(gram_done, 1)

            def squares(k):
                pe.wait_ge(n1_ready, k + 1)
                nc.tensor.matmul(inv_bank[:, 0, 0:P - 16], n1t[:], n1[:, 0:P - 16], start=True, stop=True)
                nc.tensor.matmul(inv_bank[:, 1, 16:P], n1[:], n1t[:, 16:P], start=True, stop=True).then_inc(p2_done, 1)

            def fourths(k):
                pe.wait_ge(n2_ready, k + 1)
                nc.tensor.matmul(inv_bank[:, 0, 0:P - 32], n2t[:], n2[:, 0:P - 32], start=True, stop=True)
                nc.tensor.matmul(inv_bank[:, 1, 64:P], n2[:], n2t[:, 64:P], start=True, stop=True).then_inc(p4_done, 1)

            def eighth(k):
                pe.wait_ge(n4_ready, k + 1)
                nc.tensor.matmul(inv_bank[:, 0, 64:P], n4[:], n4t[:, 64:P], start=True, stop=True).then_inc(p8_done, 1)

            def product(k, ready, left, right, first, done):
                pe.wait_ge(ready, k + 1)
                nc.tensor.matmul(inv_bank[:, 0, first:P], left[:], right[:, first:P], start=True,
                                 stop=True).then_inc(done, 1)

            def tx(k, r):
                pe.wait_ge(s0_ready, k + 1)
                pe.wait_ge(state_ready, k + 1)
                for h in range(HALVES):
                    nc.tensor.matmul(mem_bank[:, h * P:(h + 1) * P], xn[:, r, h * P:(h + 1) * P], s0[:],
                                     start=True, stop=True)
                nc.tensor.matmul(mem_bank[:, D:D + 1], s0[:], ones[:], start=True, stop=True).then_inc(tx_done, 1)

            def errors(k):
                pe.wait_ge(tx_ready, k + 1)
                for h in range(HALVES):
                    last = nc.tensor.matmul(mem_bank[:, 0:D], txt[:, h, :], state[:, h, :], start=(h == 0),
                                            stop=(h == HALVES - 1))
                last.then_inc(err_done, 1)

            def gradient(k, r):
                pe.wait_ge(err_ready, k + 1)
                for h in range(HALVES):
                    last = nc.tensor.matmul(mem_bank[:, h * D:(h + 1) * D], xn[:, r, h * P:(h + 1) * P],
                                            err[:, r, :], start=True, stop=True)
                last.then_inc(grad_done, 1)

            def experts(k, r, g):
                bank = g % EXPERT_BANKS
                if isinstance(k, int) and k == 0 and g < EXPERT_BANKS:
                    pass
                elif (g - EXPERT_BANKS) % GROUPS in ACT_GROUPS:
                    n = ACT_GROUPS.index((g - EXPERT_BANKS) % GROUPS)
                    pe.wait_ge(part_step, PS * (k if g >= EXPERT_BANKS else k - 1) + 2 * (n + 1))
                else:
                    n = DVE_GROUPS.index((g - EXPERT_BANKS) % GROUPS)
                    pe.wait_ge(z_step, ZS * (k if g >= EXPERT_BANKS else k - 1) + 2 * (n + 1))
                if isinstance(k, int) and k == 0:
                    pe.wait_ge(hi_ready, 3 + 2 * g // LOT)
                    pe.wait_ge(lo_ready, 3 + 2 * g // LOT)
                split_product(e_bank[bank][:], r, lambda h: w_hi[:, h, 2 * g:2 * g + 2, :],
                              lambda h: w_lo[:, h, 2 * g:2 * g + 2, :]).then_inc(group_done[bank], 1)

            pe.wait_ge(const_ready, 15)
            transposes(0, 0)
            pe.wait_ge(hi_ready, 2)
            pe.wait_ge(lo_ready, 2)
            values_and_logits(0, 0)
            gram(0)
            squares(0)
            fourths(0)
            eighth(0)
            product(0, s3_ready, n4, s3, 32, s2_done)
            product(0, s2_ready, n2, s2, 16, s1_done)
            product(0, s1_ready, n1, s1, 8, s0_done)

            def body(k, r):
                more = exists(k + 1)
                if more:
                    transposes(k + 1, 1 - r)
                tx(k, r)
                experts(k, r, 0)
                errors(k)
                if more:
                    values_and_logits(k + 1, 1 - r)
                    gram(k + 1)
                experts(k, r, 1)
                gradient(k, r)
                if more:
                    squares(k + 1)
                experts(k, r, 2)
                if more:
                    fourths(k + 1)
                experts(k, r, 3)
                if more:
                    eighth(k + 1)
                experts(k, r, 4)
                if more:
                    product(k + 1, s3_ready, n4, s3, 32, s2_done)
                experts(k, r, 5)
                if more:
                    product(k + 1, s2_ready, n2, s2, 16, s1_done)
                experts(k, r, 6)
                if more:
                    product(k + 1, s1_ready, n1, s1, 8, s0_done)
                experts(k, r, 7)

            in_loop(pe, body)


def kernel(L0_attn_x, L0_attn_W0, L0_attn_Wkv, L0_attn_bkv, L0_attn_eta, L0_ffn_router_w, L0_ffn_router_b,
           L0_ffn_expert_w):
    import numpy as np
    import concourse.bacc as bacc
    from concourse.bass_utils import run_bass_kernel_spmd

    def halves(w):
        return np.ascontiguousarray(np.asarray(w).reshape(HALVES, P, -1).transpose(1, 0, 2))

    x = np.asarray(L0_attn_x)
    wkv, bkv = np.asarray(L0_attn_Wkv), np.asarray(L0_attn_bkv)
    rows = x.transpose(1, 0, 2).reshape(CHUNKS, P, D).transpose(1, 0, 2)
    arrays = {
        "x_rows": np.ascontiguousarray(rows),
        "w0_t": halves(np.asarray(L0_attn_W0).T),
        "wv_router_t": halves(np.concatenate([wkv[D:].T, np.asarray(L0_ffn_router_w).T], axis=1)),
        "experts": np.ascontiguousarray(
            np.asarray(L0_ffn_expert_w).reshape(EXPERTS, HALVES, P, D).transpose(2, 1, 0, 3)),
        "bias_v": np.ascontiguousarray(bkv[D:].reshape(1, D)),
        "router_b": np.ascontiguousarray(np.asarray(L0_ffn_router_b).reshape(1, EXPERTS)),
        "eta_in": np.ascontiguousarray(np.asarray(L0_attn_eta).reshape(1, 1)),
    }
    nc = bacc.Bacc("TRN2", target_bir_lowering=False, num_devices=1)
    args = [nc.dram_tensor(n, a.shape, mybir.dt.from_np(a.dtype), kind="ExternalInput").ap()
            for n, a in arrays.items()]
    out = nc.dram_tensor("out_rows", (P, CHUNKS, D), FP32, kind="ExternalOutput").ap()
    program(nc, *args, out)
    result = run_bass_kernel_spmd(nc, [arrays], core_ids=[0])
    got = np.asarray(result.results[0]["out_rows"])
    return np.ascontiguousarray(got.transpose(1, 0, 2).reshape(STEPS, BATCH, D).transpose(1, 0, 2))
```

```python
import concourse.bass as bass
from concourse import mybir
from contextlib import ExitStack

FP32 = mybir.dt.float32
FP16 = mybir.dt.float16
FP32R = mybir.dt.float32r
INT32 = mybir.dt.int32
ALU = mybir.AluOpType
ACT = mybir.ActivationFunctionType
AX = mybir.AxisListType
ALL_ADD = bass.bass_isa.ReduceOp.add

P = 128
BATCH, STEPS, D = 8, 1024, 256
CHUNK_STEPS = P // BATCH
CHUNKS = STEPS // CHUNK_STEPS
HALVES = D // P
EXPERTS, TOP_K = 16, 6
GROUPS = EXPERTS // 2
EXPERT_BANKS = 4
LN_EPS, EPS = 1e-5, 1e-10
VR = D + EXPERTS
X_SCALE = 256.0
W_TOP = 16384.0
W_LOTS = 4
LOT = EXPERTS // W_LOTS
HEAD = 3
FIRST, LAST = 2, 4
ACT_GROUPS = (1, 5)
DVE_GROUPS = tuple(g for g in range(GROUPS) if g not in ACT_GROUPS)
ZS = 2 * len(DVE_GROUPS)
PS = 2 * len(ACT_GROUPS)
MAGIC = 0x5F3759DF
EXPONENT = 0x7F800000


def program(nc, x_in, w0t_in, wvr_in, expert_in, b_in, rb_in, eta_in, out):
    ctx = ExitStack()
    with ctx:
        def sb(name, shape, dt=FP32):
            return ctx.enter_context(nc.sbuf_tensor(name, shape, dt))

        def pb(name, shape):
            return ctx.enter_context(nc.psum_tensor(name, shape, FP32))

        def sem(name):
            return ctx.enter_context(nc.semaphore(name))

        x_all = sb("x_all", [P, CHUNKS, D])
        w_raw = sb("w_raw", [P, HALVES, EXPERTS, D])
        w_hi = sb("w_hi", [P, HALVES, EXPERTS, D], FP16)
        w_lo = sb("w_lo", [P, HALVES, EXPERTS, D], FP16)
        vr_raw = sb("vr_raw", [P, HALVES, VR])
        vr_hi = sb("vr_hi", [P, HALVES, VR], FP16)
        vr_lo = sb("vr_lo", [P, HALVES, VR], FP16)
        state = sb("state", [P, HALVES, D])
        b_row = sb("b_row", [P, D])
        rb_row = sb("rb_row", [P, EXPERTS])
        eta = sb("eta", [P, 1])
        neg_c = sb("neg_c", [P, 1])
        ident = sb("ident", [P, P])
        ones = sb("ones", [P, 1])
        lower = sb("lower", [P, P])
        upper = sb("upper", [P, P])
        squares_p = sb("squares_p", [P, 2 + W_LOTS])
        squares_all = sb("squares_all", [P, 2 + W_LOTS])
        clamped = sb("clamped", [P, 2 + W_LOTS])
        halved = sb("halved", [P, 2 + W_LOTS], INT32)
        shifted = sb("shifted", [P, 2 + W_LOTS], INT32)
        c_pos = sb("c_pos", [P, 1])
        power = sb("power", [P, 2 + W_LOTS])
        rpower = sb("rpower", [P, 2 + W_LOTS])
        scale = sb("scale", [P, 2 + W_LOTS])
        unscale = sb("unscale", [P, 2 + W_LOTS])
        un_e = sb("un_e", [P, EXPERTS])
        q = sb("q", [P, 1])
        half_unq = sb("half_unq", [P, 1])

        stats = sb("stats", [P, 2, 6])
        mv = sb("mv", [P, 2, 2])
        vare = sb("vare", [P, 2, 1])
        nvh = sb("nvh", [P, 2, 1])
        half_bits = sb("half_bits", [P, 2, 1], INT32)
        rs = [sb(f"rs{n}", [P, 2, 1]) for n in range(4)]
        nt_a = sb("nt_a", [P, 2, 3])
        nt_b = sb("nt_b", [P, 2, 3])
        nt_c = sb("nt_c", [P, 2, 3])
        neg_half = sb("neg_half", [P, 1])
        three_halves = sb("three_halves", [P, 1])
        xn = sb("xn", [P, 2, D])
        xt = sb("xt", [P, HALVES, P])
        xt_hi = sb("xt_hi", [P, 2, HALVES, P], FP16)
        xt_lo = sb("xt_lo", [P, 2, HALVES, P], FP16)
        n1 = sb("n1", [P, P])
        n1t = sb("n1t", [P, P])
        n2 = sb("n2", [P, P])
        n2t = sb("n2t", [P, P])
        n4 = sb("n4", [P, P])
        n4t = sb("n4t", [P, P])
        s3 = sb("s3", [P, P])
        s2 = sb("s2", [P, P])
        s1 = sb("s1", [P, P])
        s0 = sb("s0", [P, P])
        tx_hi = sb("tx_hi", [P, HALVES, P], FP32R)
        tx_lo = sb("tx_lo", [P, HALVES, P], FP32R)
        xn_hi = sb("xn_hi", [P, D], FP32R)
        xn_lo = sb("xn_lo", [P, D], FP32R)
        err_hi = sb("err_hi", [P, D], FP32R)
        err_lo = sb("err_lo", [P, D], FP32R)
        state_hi = sb("state_hi", [P, HALVES, D], FP32R)
        state_lo = sb("state_lo", [P, HALVES, D], FP32R)
        neg_t1 = sb("neg_t1", [P, 1])
        err = sb("err", [P, 2, D])
        v = sb("v", [P, 2, D])
        y = sb("y", [P, 2, D])
        logit = sb("logit", [P, 2, EXPERTS])
        top_l = sb("top_l", [P, 2, 8])
        neg_max = sb("neg_max", [P, 2, 1])
        ex = sb("ex", [P, 2, EXPERTS + 2])
        ex_sum = sb("ex_sum", [P, 2, 1])
        top_e = sb("top_e", [P, 2, 8])
        rest = sb("rest", [P, 2, EXPERTS + 2])
        ex_eps = sb("ex_eps", [P, 2, 1])
        sel = sb("sel", [P, 2, EXPERTS])
        sel_sum = sb("sel_sum", [P, 2, 1])
        denom = sb("denom", [P, 2, 1])
        rdenom = sb("rdenom", [P, 2, 1])
        eps_term = sb("eps_term", [P, 2, 1])
        acc = sb("acc", [P, 2, 1])
        racc = sb("racc", [P, 2, 1])
        factor = sb("factor", [P, 2, 1])
        gate = sb("gate", [P, 2, EXPERTS])
        zacc = sb("zacc", [P, 2, 2, D])
        part = sb("part", [P, 2, PS, D])
        psum01 = sb("psum01", [P, D])
        psum23 = sb("psum23", [P, D])
        parts = sb("parts", [P, D])
        zeo = sb("zeo", [P, D])
        z = sb("z", [P, 2, D])
        th = sb("th", [P, 2, D])
        zt = sb("zt", [P, D])
        silu2 = sb("silu2", [P, 2, D])
        sg = sb("sg", [P, 2, D])

        t_bank = pb("t_bank", [P, HALVES, D])
        vr_bank = pb("vr_bank", [P, 512])
        inv_bank = pb("inv_bank", [P, 4, P])
        mem_bank = pb("mem_bank", [P, 512])
        e_bank = [pb(f"e_bank{n}", [P, 512]) for n in range(EXPERT_BANKS)]

        x_loaded = sem("x_loaded")
        small_loaded = sem("small_loaded")
        vr_loaded = sem("vr_loaded")
        w_loaded = [sem(f"w_loaded{n}") for n in range(W_LOTS)]
        stored = sem("stored")
        const_ready = sem("const_ready")
        mask_scaled = sem("mask_scaled")
        squares_ready = sem("squares_ready")
        all_ready = sem("all_ready")
        scale_ready = sem("scale_ready")
        hi_ready = sem("hi_ready")
        lo_ready = sem("lo_ready")
        setup_step = sem("setup_step")
        setup_pool = sem("setup_pool")
        state_ready = sem("state_ready")
        state_high = sem("state_high")
        state_low = sem("state_low")
        rows_high = sem("rows_high")
        rows_low = sem("rows_low")
        err_high = sem("err_high")
        err_low = sem("err_low")
        tx_low = sem("tx_low")
        stat_step = sem("stat_step")
        newton = sem("newton")
        xn_ready = sem("xn_ready")
        transposed = sem("transposed")
        xh_ready = sem("xh_ready")
        xt_ready = sem("xt_ready")
        xl_ready = sem("xl_ready")
        vr_done = sem("vr_done")
        v_ready = sem("v_ready")
        route = sem("route")
        ex_ready = sem("ex_ready")
        gram_done = sem("gram_done")
        n1_ready = sem("n1_ready")
        p2_done = sem("p2_done")
        n2_ready = sem("n2_ready")
        p4_done = sem("p4_done")
        n4_ready = sem("n4_ready")
        p8_done = sem("p8_done")
        s3_ready = sem("s3_ready")
        s2_done = sem("s2_done")
        s2_ready = sem("s2_ready")
        s1_done = sem("s1_done")
        s1_ready = sem("s1_ready")
        s0_done = sem("s0_done")
        s0_ready = sem("s0_ready")
        tx_done = sem("tx_done")
        tx_ready = sem("tx_ready")
        err_done = sem("err_done")
        err_ready = sem("err_ready")
        grad_done = sem("grad_done")
        group_done = [sem(f"group_done{n}") for n in range(EXPERT_BANKS)]
        z_step = sem("z_step")
        part_step = sem("part_step")
        part_sum = sem("part_sum")
        z_sum = sem("z_sum")
        y_ready = sem("y_ready")
        th_ready = sem("th_ready")
        zt_ready = sem("zt_ready")
        silu_ready = sem("silu_ready")
        sg_ready = sem("sg_ready")
        out_ready = sem("out_ready")
        ROUTE, STAT, NEWTON = 15, 5, 13

        def past(k, n):
            return not isinstance(k, int) or k >= n

        def in_loop(eng, body):
            for k in range(FIRST):
                body(k, k % 2)
            with eng.Fori(0, (CHUNKS - FIRST - LAST) // 2) as pair:
                for r in range(2):
                    body(2 * pair + (FIRST + r), r)
            for k in range(CHUNKS - LAST, CHUNKS):
                body(k, k % 2)

        def exists(k):
            return not isinstance(k, int) or k < CHUNKS

        block = ctx.enter_context(nc.Block())

        @block.sync
        def _(sp):
            sp.dma_start(x_all[:, 0:HEAD, :], x_in[:, 0:HEAD, :]).then_inc(x_loaded, 16)
            with sp.Fori(HEAD, CHUNKS) as k:
                sp.wait_ge(x_loaded, 16 * (k - (HEAD - 1)))
                sp.dma_start(x_all[:, k, :], x_in[:, k, :]).then_inc(x_loaded, 16)
            with sp.Fori(0, CHUNKS) as k:
                sp.wait_ge(out_ready, k + 1)
                sp.dma_start(out[:, k, :], x_all[:, k, :]).then_inc(stored, 16)
            sp.wait_ge(stored, 16 * CHUNKS)

        @block.gpsimd
        def _(pool):
            nc.gpsimd.memset(ident[:], 0.0).then_inc(setup_pool, 1)
            nc.gpsimd.memset(lower[:], 1.0).then_inc(setup_pool, 1)
            nc.gpsimd.memset(upper[:], 1.0).then_inc(setup_pool, 1)
            pool.wait_ge(setup_pool, 3)
            nc.gpsimd.affine_select(out=ident[:], in_=ident[:], compare_op=ALU.not_equal, fill=1.0, base=0,
                                    pattern=[[-1, P]], channel_multiplier=1).then_inc(const_ready, 1)
            low3 = lower[:].rearrange("p (j r) -> p j r", r=BATCH)
            upp3 = upper[:].rearrange("p (j r) -> p j r", r=BATCH)
            nc.gpsimd.affine_select(out=low3, in_=low3, compare_op=ALU.is_ge, fill=0.0, base=-BATCH,
                                    pattern=[[-BATCH, CHUNK_STEPS], [0, BATCH]],
                                    channel_multiplier=1).then_inc(const_ready, 1)
            nc.gpsimd.affine_select(out=upp3, in_=upp3, compare_op=ALU.is_ge, fill=0.0, base=-1,
                                    pattern=[[BATCH, CHUNK_STEPS], [0, BATCH]],
                                    channel_multiplier=-1).then_inc(const_ready, 1)
            nc.gpsimd.memset(ones[:], 1.0).then_inc(const_ready, 1)
            nc.gpsimd.memset(neg_half[:], -0.5).then_inc(const_ready, 1)
            nc.gpsimd.memset(three_halves[:], 1.5).then_inc(const_ready, 1)
            nc.gpsimd.memset(ex[:], -1.0).then_inc(const_ready, 1)
            for t in (n2, n2t, n4, n4t):
                nc.gpsimd.memset(t[:], 0.0).then_inc(const_ready, 1)
            pool.wait_ge(const_ready, 1)
            for t in (s3, s2, s1, s0):
                nc.gpsimd.tensor_copy(t[:], ident[:]).then_inc(const_ready, 1)

            def newton_steps(k, r):
                pool.wait_ge(stat_step, STAT * (k + 1))
                base = NEWTON * k
                nc.gpsimd.tensor_tensor(nvh[:, r, :], vare[:, r, :], neg_half[:], ALU.mult).then_inc(newton, 1)
                for n in range(3):
                    guess, a, b, c = rs[n][:, r, :], nt_a[:, r, n:n + 1], nt_b[:, r, n:n + 1], nt_c[:, r, n:n + 1]
                    nc.gpsimd.tensor_tensor(a, guess, guess, ALU.mult).then_inc(newton, 1)
                    pool.wait_ge(newton, base + (4 * n + 2))
                    nc.gpsimd.tensor_tensor(b, a, nvh[:, r, :], ALU.mult).then_inc(newton, 1)
                    pool.wait_ge(newton, base + (4 * n + 3))
                    nc.gpsimd.tensor_tensor(c, b, three_halves[:], ALU.add).then_inc(newton, 1)
                    pool.wait_ge(newton, base + (4 * n + 4))
                    if n == 2 and past(k, 2):
                        pool.wait_ge(xn_ready, k - 1)
                    nc.gpsimd.tensor_tensor(rs[n + 1][:, r, :], guess, c, ALU.mult).then_inc(newton, 1)
                    if n < 2:
                        pool.wait_ge(newton, base + (4 * n + 5))

            pool.wait_ge(const_ready, 7)
            newton_steps(0, 0)
            newton_steps(1, 1)
            for n in range(2 + W_LOTS):
                pool.wait_ge(squares_ready, n + 1)
                nc.gpsimd.partition_all_reduce(squares_all[:, n:n + 1], squares_p[:, n:n + 1], P,
                                               ALL_ADD).then_inc(all_ready, 1)
                if n == 2:
                    newton_steps(2, 0)

            def z_total(k, r):
                pool.wait_ge(z_step, ZS * (k + 1))
                nc.gpsimd.tensor_tensor(zeo[:], zacc[:, r, 0, :], zacc[:, r, 1, :], ALU.add).then_inc(z_sum, 1)
                pool.wait_ge(part_sum, 3 * (k + 1))
                pool.wait_ge(z_sum, 2 * k + 1)
                if past(k, 2):
                    pool.wait_ge(th_ready, k - 1)
                nc.gpsimd.tensor_tensor(z[:, r, :], zeo[:], parts[:], ALU.add).then_inc(z_sum, 1)

            def silu_of(k, r):
                pool.wait_ge(th_ready, k + 1)
                nc.gpsimd.tensor_tensor(zt[:], z[:, r, :], th[:, r, :], ALU.mult).then_inc(zt_ready, 1)
                pool.wait_ge(zt_ready, k + 1)
                if past(k, 2):
                    pool.wait_ge(sg_ready, k - 1)
                nc.gpsimd.tensor_tensor(silu2[:, r, :], z[:, r, :], zt[:], ALU.add).then_inc(silu_ready, 1)

            def low_rows(k, r):
                pool.wait_ge(rows_high, k + 1)
                nc.gpsimd.tensor_tensor(xn_lo[:], xn[:, r, :], xn_hi[:].bitcast(FP32),
                                        ALU.subtract).then_inc(rows_low, 1)

            def result(k, r):
                pool.wait_ge(sg_ready, k + 1)
                nc.gpsimd.tensor_tensor(x_all[:, k, :], sg[:, r, :], x_all[:, k, :],
                                        ALU.add).then_inc(out_ready, 1)

            def body(k, r):
                low_rows(k, r)
                if past(k, 1):
                    z_total(k - 1, 1 - r)
                    silu_of(k - 1, 1 - r)
                pool.wait_ge(err_ready, k + 1)
                pool.wait_ge(v_ready, k + 1)
                if past(k, 2):
                    pool.wait_ge(sg_ready, k - 1)
                nc.gpsimd.tensor_tensor(y[:, r, :], err[:, r, :], v[:, r, :], ALU.add).then_inc(y_ready, 1)
                pool.wait_ge(part_step, PS * k + 2)
                if past(k, 1):
                    pool.wait_ge(part_sum, 3 * k)
                nc.gpsimd.tensor_tensor(psum01[:], part[:, r, 0, :], part[:, r, 1, :],
                                        ALU.add).then_inc(part_sum, 1)
                if past(k, 1):
                    result(k - 1, 1 - r)
                if exists(k + 3):
                    newton_steps(k + 3, 1 - r)
                pool.wait_ge(part_step, PS * k + 4)
                nc.gpsimd.tensor_tensor(psum23[:], part[:, r, 2, :], part[:, r, 3, :],
                                        ALU.add).then_inc(part_sum, 1)
                pool.wait_ge(part_sum, 3 * k + 2)
                if past(k, 1):
                    pool.wait_ge(z_sum, 2 * k)
                nc.gpsimd.tensor_tensor(parts[:], psum01[:], psum23[:], ALU.add).then_inc(part_sum, 1)

            in_loop(pool, body)

        @block.scalar
        def _(act):
            act.dma_start(vr_raw[:], wvr_in).then_inc(vr_loaded, 16)
            act.dma_start(state[:], w0t_in).then_inc(small_loaded, 16)
            act.dma_start(b_row[:], b_in.broadcast_to([P, D])).then_inc(small_loaded, 16)
            act.dma_start(rb_row[:], rb_in.broadcast_to([P, EXPERTS])).then_inc(small_loaded, 16)
            act.dma_start(eta[:], eta_in.broadcast_to([P, 1])).then_inc(small_loaded, 16)
            for n in range(W_LOTS):
                act.dma_start(w_raw[:, :, n * LOT:(n + 1) * LOT, :],
                              expert_in[:, :, n * LOT:(n + 1) * LOT, :]).then_inc(w_loaded[n], 16)

            def high_parts(k, r):
                act.wait_ge(transposed, k + 1)
                if past(k, 2):
                    act.wait_ge(group_done[EXPERT_BANKS - 1], 2 * (k - 1))
                nc.scalar.activation(xt_hi[:, r, :, :], t_bank[:, :, 0:P], ACT.Copy,
                                     scale=X_SCALE).then_inc(xh_ready, 1)

            def transposed_out(k):
                if past(k, 1):
                    act.wait_ge(gram_done, k)
                nc.scalar.activation(xt[:], t_bank[:, :, 0:P], ACT.Copy).then_inc(xt_ready, 1)

            def tx_out(k, r):
                act.wait_ge(tx_done, k + 1)
                if past(k, 1):
                    act.wait_ge(err_ready, k)
                nc.scalar.activation(tx_hi[:], mem_bank[:, 0:D].rearrange("p (h t) -> p h t", h=HALVES), ACT.Copy)
                nc.scalar.activation(neg_t1[:], mem_bank[:, D:D + 1], ACT.Copy, scale=-1.0).then_inc(tx_ready, 1)

            def high_rows(k, r):
                if past(k, 1):
                    act.wait_ge(grad_done, k)
                    act.wait_ge(rows_low, k)
                act.wait_ge(xn_ready, k + 1)
                nc.scalar.activation(xn_hi[:], xn[:, r, :], ACT.Copy).then_inc(rows_high, 1)

            def high_err(k, r):
                act.wait_ge(err_ready, k + 1)
                nc.scalar.activation(err_hi[:], err[:, r, :], ACT.Copy).then_inc(err_high, 1)

            def high_state(k):
                act.wait_ge(state_ready, k + 1)
                nc.scalar.activation(state_hi[:], state[:], ACT.Copy).then_inc(state_high, 1)

            def group(k, r, n):
                g = ACT_GROUPS[n]
                bank = g % EXPERT_BANKS
                act.wait_ge(group_done[bank], 2 * k + (g // EXPERT_BANKS + 1))
                if n == 0:
                    act.wait_ge(route, ROUTE * (k + 1))
                    if past(k, 2):
                        act.wait_ge(part_sum, 3 * (k - 1))
                for j in range(2):
                    e = 2 * g + j
                    nc.scalar.activation(part[:, r, 2 * n + j, :], e_bank[bank][:, j * D:(j + 1) * D], ACT.Copy,
                                         scale=gate[:, r, e:e + 1]).then_inc(part_step, 1)

            def squares(k):
                act.wait_ge(p2_done, k + 1)
                nc.scalar.activation(n2[:, 0:P - 16], inv_bank[:, 0, 0:P - 16], ACT.Copy)
                nc.scalar.activation(n2t[:, 16:P], inv_bank[:, 1, 16:P], ACT.Copy).then_inc(n2_ready, 1)

            def fourths(k):
                act.wait_ge(p4_done, k + 1)
                nc.scalar.activation(n4[:, 0:P - 32], inv_bank[:, 0, 0:P - 32], ACT.Copy)
                nc.scalar.activation(n4t[:, 64:P], inv_bank[:, 1, 64:P], ACT.Copy).then_inc(n4_ready, 1)

            def exponent(k, r):
                act.wait_ge(route, ROUTE * k + 3)
                nc.scalar.activation(ex[:, r, 0:EXPERTS], logit[:, r, :], ACT.Exp, bias=neg_max[:, r, :],
                                     accum_out=ex_sum[:, r, :]).then_inc(ex_ready, 1)

            def tanh_of(k, r):
                act.wait_ge(z_sum, 2 * (k + 1))
                if past(k, 2):
                    act.wait_ge(silu_ready, k - 1)
                nc.scalar.activation(th[:, r, :], z[:, r, :], ACT.Tanh, scale=0.5).then_inc(th_ready, 1)

            def lot_squares(n):
                act.wait_ge(w_loaded[n], 16)
                lot = slice(n * LOT, (n + 1) * LOT)
                nc.scalar.activation(w_lo[:, :, lot, :].rearrange("p h e d -> p h (e d)"),
                                     w_raw[:, :, lot, :].rearrange("p h e d -> p h (e d)"), ACT.Square,
                                     accum_out=squares_p[:, 2 + n:3 + n]).then_inc(squares_ready, 1)

            def lot_high(n):
                act.wait_ge(scale_ready, 2)
                lot = slice(n * LOT, (n + 1) * LOT)
                nc.scalar.activation(w_hi[:, :, lot, :].rearrange("p h e d -> p h (e d)"),
                                     w_raw[:, :, lot, :].rearrange("p h e d -> p h (e d)"), ACT.Copy,
                                     scale=scale[:, 2 + n:3 + n]).then_inc(hi_ready, 1)

            act.wait_ge(vr_loaded, 16)
            nc.scalar.activation(vr_lo[:, :, 0:D], vr_raw[:, :, 0:D], ACT.Square,
                                 accum_out=squares_p[:, 0:1]).then_inc(squares_ready, 1)
            nc.scalar.activation(vr_lo[:, :, D:VR], vr_raw[:, :, D:VR], ACT.Square,
                                 accum_out=squares_p[:, 1:2]).then_inc(squares_ready, 1)
            lot_squares(0)
            act.wait_ge(scale_ready, 1)
            nc.scalar.activation(vr_hi[:, :, 0:D], vr_raw[:, :, 0:D], ACT.Copy, scale=scale[:, 0:1]).then_inc(hi_ready, 1)
            nc.scalar.activation(vr_hi[:, :, D:VR], vr_raw[:, :, D:VR], ACT.Copy,
                                 scale=scale[:, 1:2]).then_inc(hi_ready, 1)
            act.wait_ge(const_ready, 15)
            high_parts(0, 0)
            transposed_out(0)
            for n in range(1, W_LOTS):
                lot_squares(n)
            squares(0)
            exponent(0, 0)
            fourths(0)
            lot_high(0)

            def body(k, r):
                if exists(k + 1):
                    high_parts(k + 1, 1 - r)
                tx_out(k, r)
                if exists(k + 1):
                    transposed_out(k + 1)
                high_rows(k, r)
                if not past(k, 1):
                    lot_high(1)
                high_err(k, r)
                if not past(k, 1):
                    lot_high(2)
                    lot_high(3)
                if past(k, 1):
                    tanh_of(k - 1, 1 - r)
                group(k, r, 0)
                if exists(k + 1):
                    squares(k + 1)
                    exponent(k + 1, 1 - r)
                high_state(k)
                if exists(k + 1):
                    fourths(k + 1)
                group(k, r, 1)

            in_loop(act, body)
            last = CHUNKS - 1
            tanh_of(last, last % 2)

        @block.vector
        def _(dve):
            def stats_waits(k):
                dve.wait_ge(x_loaded, 16 if isinstance(k, int) and k < HEAD else 16 * (k - (HEAD - 2)))

            def stats_first(k, r):
                nc.vector.bn_stats(stats[:, r, :], x_all[:, k, :]).then_inc(stat_step, 1)

            def stats_second_waits(k):
                if past(k, 2):
                    dve.wait_ge(xn_ready, k - 1)
                dve.wait_ge(stat_step, STAT * k + 1)

            def stats_second(k, r):
                nc.vector.bn_aggr(mv[:, r, :], stats[:, r, :]).then_inc(stat_step, 1)

            def guess_of(k, r):
                base = STAT * k
                dve.wait_ge(stat_step, base + 2)
                nc.vector.tensor_scalar(vare[:, r, :], mv[:, r, 1:2], LN_EPS, None, ALU.add).then_inc(stat_step, 1)
                dve.wait_ge(stat_step, base + 3)
                nc.vector.tensor_scalar(half_bits[:, r, :], vare[:, r, :].bitcast(INT32), 1, None,
                                        ALU.logical_shift_right).then_inc(stat_step, 1)
                dve.wait_ge(stat_step, base + 4)
                nc.vector.tensor_scalar(rs[0][:, r, :].bitcast(INT32), half_bits[:, r, :], -1.0, float(MAGIC),
                                        ALU.mult, ALU.add).then_inc(stat_step, 1)

            def stats_of(k, r):
                stats_waits(k)
                stats_first(k, r)
                stats_second_waits(k)
                stats_second(k, r)
                guess_of(k, r)

            def normalize(k, r):
                dve.wait_ge(newton, NEWTON * (k + 1))
                if past(k, 2):
                    dve.wait_ge(grad_done, k - 1)
                nc.vector.tensor_scalar(xn[:, r, :], x_all[:, k, :], mv[:, r, 0:1], rs[3][:, r, :],
                                        ALU.subtract, ALU.mult).then_inc(xn_ready, 1)

            steps = [0]

            def link(ins):
                steps[0] += 1
                ins.then_inc(setup_step, 1)
                dve.wait_ge(setup_step, steps[0])

            def scales_of(first, last):
                dve.wait_ge(all_ready, last)
                c = slice(first, last)
                link(nc.vector.tensor_scalar(clamped[:, c], squares_all[:, c], 2.0 ** -40, None, ALU.max))
                link(nc.vector.tensor_scalar(halved[:, c], clamped[:, c].bitcast(INT32), 1, None,
                                             ALU.logical_shift_right))
                link(nc.vector.tensor_scalar(shifted[:, c], halved[:, c], float(129 << 22), None, ALU.add))
                link(nc.vector.tensor_scalar(power[:, c].bitcast(INT32), shifted[:, c], EXPONENT, None,
                                             ALU.bitwise_and))
                link(nc.vector.reciprocal(rpower[:, c], power[:, c]))
                link(nc.vector.tensor_scalar(unscale[:, c], power[:, c], 1.0 / (W_TOP * X_SCALE), None, ALU.mult))
                nc.vector.tensor_scalar(scale[:, c], rpower[:, c], W_TOP, None, ALU.mult).then_inc(scale_ready, 1)

            def lot_low(n):
                lot = slice(n * LOT, (n + 1) * LOT)
                dve.wait_ge(hi_ready, 3 + n)
                nc.vector.scalar_tensor_tensor(
                    out=w_lo[:, :, lot, :].rearrange("p h e d -> p h (e d)"),
                    in0=w_raw[:, :, lot, :].rearrange("p h e d -> p h (e d)"), scalar=scale[:, 2 + n:3 + n],
                    in1=w_hi[:, :, lot, :].rearrange("p h e d -> p h (e d)"), op0=ALU.mult,
                    op1=ALU.subtract).then_inc(lo_ready, 1)

            def low_parts(k, r):
                dve.wait_ge(xh_ready, k + 1)
                if past(k, 1):
                    dve.wait_ge(group_done[EXPERT_BANKS - 1], 2 * (k - 1)) if past(k, 2) else None
                dve.wait_ge(xt_ready, k + 1)
                nc.vector.scalar_tensor_tensor(out=xt_lo[:, r, :, :], in0=t_bank[:, :, 0:P], scalar=X_SCALE,
                                               in1=xt_hi[:, r, :, :], op0=ALU.mult,
                                               op1=ALU.subtract).then_inc(xl_ready, 1)

            def gram_out(k):
                dve.wait_ge(gram_done, k + 1)
                nc.vector.tensor_tensor(n1[:], inv_bank[:, 0, :], lower[:], ALU.mult)
                nc.vector.tensor_tensor(n1t[:], inv_bank[:, 0, :], upper[:], ALU.mult).then_inc(n1_ready, 1)

            def logits_out(k, r):
                dve.wait_ge(vr_done, k + 1)
                base = ROUTE * k
                nc.vector.scalar_tensor_tensor(out=logit[:, r, :], in0=vr_bank[:, D:VR], scalar=unscale[:, 1:2],
                                               in1=rb_row[:], op0=ALU.mult, op1=ALU.add).then_inc(route, 1)
                if past(k, 2):
                    dve.wait_ge(y_ready, k - 1)
                nc.vector.tensor_tensor(v[:, r, :], vr_bank[:, 0:D], b_row[:], ALU.add).then_inc(v_ready, 1)

            def top_logit_waits(k):
                dve.wait_ge(route, ROUTE * k + 1)

            def top_logit(k, r):
                base = ROUTE * k
                nc.vector.max(top_l[:, r, :], logit[:, r, :]).then_inc(route, 1)
                dve.wait_ge(route, base + 2)
                nc.vector.tensor_scalar(neg_max[:, r, :], top_l[:, r, 0:1], -1.0, None, ALU.mult).then_inc(route, 1)

            def top_gates(k, r):
                base = ROUTE * k
                nc.vector.max(top_e[:, r, :], ex[:, r, 0:EXPERTS]).then_inc(route, 1)
                dve.wait_ge(route, base + 4)
                nc.vector.memset(top_e[:, r, TOP_K:8], -1.0).then_inc(route, 1)
                dve.wait_ge(route, base + 5)
                nc.vector.tensor_scalar(ex_eps[:, r, :], ex_sum[:, r, :], EPS, None, ALU.mult).then_inc(route, 1)
                nc.vector.match_replace(rest[:, r, :], top_e[:, r, :], ex[:, r, :], 0.0).then_inc(route, 1)
                dve.wait_ge(route, base + 7)
                nc.vector.scalar_tensor_tensor(out=sel[:, r, :], in0=ex[:, r, 0:EXPERTS], scalar=1.0,
                                               in1=rest[:, r, 0:EXPERTS], op0=ALU.mult, op1=ALU.subtract,
                                               accum_out=sel_sum[:, r, :]).then_inc(route, 1)

            def gates_norm(k, r):
                base = ROUTE * k
                dve.wait_ge(route, base + 8)
                nc.vector.tensor_tensor(denom[:, r, :], ex_eps[:, r, :], sel_sum[:, r, :], ALU.add).then_inc(route, 1)
                dve.wait_ge(route, base + 9)
                nc.vector.reciprocal(rdenom[:, r, :], denom[:, r, :]).then_inc(route, 1)
                dve.wait_ge(route, base + 10)
                nc.vector.tensor_scalar(acc[:, r, :], sel_sum[:, r, :], rdenom[:, r, :], EPS, ALU.mult,
                                        ALU.max).then_inc(route, 1)
                nc.vector.tensor_scalar(eps_term[:, r, :], sel_sum[:, r, :], rdenom[:, r, :], EPS, ALU.mult,
                                        ALU.mult).then_inc(route, 1)

            def gates_scaled(k, r):
                base = ROUTE * k
                dve.wait_ge(route, base + 11)
                nc.vector.reciprocal(racc[:, r, :], acc[:, r, :]).then_inc(route, 1)
                dve.wait_ge(route, base + 13)
                nc.vector.tensor_tensor(factor[:, r, :], rdenom[:, r, :], racc[:, r, :], ALU.mult).then_inc(route, 1)
                dve.wait_ge(route, base + 14)
                if past(k, 2):
                    dve.wait_ge(part_step, PS * (k - 1))
                nc.vector.scalar_tensor_tensor(out=gate[:, r, :], in0=sel[:, r, :], scalar=factor[:, r, :],
                                               in1=un_e[:], op0=ALU.mult, op1=ALU.mult).then_inc(route, 1)

            def identity_plus_eighth(k):
                dve.wait_ge(p8_done, k + 1)
                nc.vector.tensor_tensor(s3[:, 64:P], inv_bank[:, 0, 64:P], ident[:, 64:P], ALU.add).then_inc(s3_ready, 1)

            def add_product(k, done, dst, src, first, op, ready):
                dve.wait_ge(done, k + 1)
                nc.vector.tensor_tensor(dst[:, first:P], src[:, first:P], inv_bank[:, 0, first:P], op).then_inc(ready, 1)

            def low_tx(k):
                dve.wait_ge(tx_ready, k + 1)
                nc.vector.tensor_tensor(tx_lo[:], mem_bank[:, 0:D].rearrange("p (h t) -> p h t", h=HALVES),
                                        tx_hi[:].bitcast(FP32), ALU.subtract).then_inc(tx_low, 1)

            def low_err(k, r):
                dve.wait_ge(err_high, k + 1)
                nc.vector.tensor_tensor(err_lo[:], err[:, r, :], err_hi[:].bitcast(FP32),
                                        ALU.subtract).then_inc(err_low, 1)

            def low_state(k):
                dve.wait_ge(state_high, k + 1)
                nc.vector.tensor_tensor(state_lo[:], state[:], state_hi[:].bitcast(FP32),
                                        ALU.subtract).then_inc(state_low, 1)

            def err_out(k, r):
                dve.wait_ge(err_done, k + 1)
                dve.wait_ge(tx_ready, k + 1)
                if past(k, 2):
                    dve.wait_ge(y_ready, k - 1)
                nc.vector.scalar_tensor_tensor(out=err[:, r, :], in0=b_row[:], scalar=neg_t1[:], in1=mem_bank[:, 0:D],
                                               op0=ALU.mult, op1=ALU.add).then_inc(err_ready, 1)

            def update(k):
                dve.wait_ge(grad_done, k + 1)
                flat = state[:].rearrange("p h e -> p (h e)")
                nc.vector.scalar_tensor_tensor(out=flat, in0=mem_bank[:], scalar=neg_c[:], in1=flat,
                                               op0=ALU.mult, op1=ALU.add).then_inc(state_ready, 1)

            def group(k, r, n):
                g = DVE_GROUPS[n]
                bank = g % EXPERT_BANKS
                base = ZS * k
                dve.wait_ge(group_done[bank], 2 * k + (g // EXPERT_BANKS + 1))
                if n == 0:
                    dve.wait_ge(route, ROUTE * (k + 1))
                    if past(k, 2):
                        dve.wait_ge(z_sum, 2 * (k - 1))
                for j in range(2):
                    e = 2 * g + j
                    src = e_bank[bank][:, j * D:(j + 1) * D]
                    if n == 0:
                        nc.vector.tensor_scalar(zacc[:, r, j, :], src, gate[:, r, e:e + 1],
                                                None if j else eps_term[:, r, :], ALU.mult,
                                                ALU.bypass if j else ALU.add).then_inc(z_step, 1)
                    else:
                        dve.wait_ge(z_step, base + (2 * n + j - 1))
                        nc.vector.scalar_tensor_tensor(out=zacc[:, r, j, :], in0=src, scalar=gate[:, r, e:e + 1],
                                                       in1=zacc[:, r, j, :], op0=ALU.mult,
                                                       op1=ALU.add).then_inc(z_step, 1)

            def gated(k, r):
                dve.wait_ge(silu_ready, k + 1)
                dve.wait_ge(y_ready, k + 1)
                if past(k, 2):
                    dve.wait_ge(out_ready, k - 1)
                nc.vector.scalar_tensor_tensor(out=sg[:, r, :], in0=silu2[:, r, :], scalar=half_unq[:],
                                               in1=y[:, r, :], op0=ALU.mult, op1=ALU.mult).then_inc(sg_ready, 1)

            for k in range(2):
                stats_of(k, k)
            for k in range(2):
                normalize(k, k)
            stats_of(2, 0)
            dve.wait_ge(small_loaded, 64)
            link(nc.vector.tensor_scalar(neg_c[:], eta[:], -2.0 / (BATCH * D), None, ALU.mult))
            dve.wait_ge(const_ready, 3)
            link(nc.vector.tensor_scalar(c_pos[:], neg_c[:], -1.0, None, ALU.mult))
            nc.vector.tensor_scalar(lower[:], lower[:], c_pos[:], None, ALU.mult).then_inc(mask_scaled, 1)
            nc.vector.tensor_scalar(upper[:], upper[:], c_pos[:], None, ALU.mult).then_inc(mask_scaled, 1)
            dve.wait_ge(vr_loaded, 16)
            link(nc.vector.tensor_tensor(state[:], state[:], vr_raw[:, :, 0:D], ALU.subtract))
            scales_of(0, 2)
            for n, c in ((0, slice(0, D)), (1, slice(D, VR))):
                dve.wait_ge(hi_ready, n + 1)
                nc.vector.scalar_tensor_tensor(out=vr_lo[:, :, c], in0=vr_raw[:, :, c], scalar=scale[:, n:n + 1],
                                               in1=vr_hi[:, :, c], op0=ALU.mult, op1=ALU.subtract).then_inc(lo_ready, 1)
            link(nc.vector.tensor_scalar(q[:], scale[:, 0:1], X_SCALE, None, ALU.mult))
            nc.vector.tensor_scalar(half_unq[:], unscale[:, 0:1], 0.5, None, ALU.mult)
            nc.vector.tensor_scalar(b_row[:], b_row[:], q[:], None, ALU.mult).then_inc(setup_step, 1)
            steps[0] += 1
            link(nc.vector.tensor_scalar(state[:], state[:], q[:], None, ALU.mult))
            nc.vector.tensor_copy(state_hi[:], state[:]).then_inc(state_high, 1)
            low_state(0)

            dve.wait_ge(mask_scaled, 2)
            dve.wait_ge(const_ready, 15)
            low_parts(0, 0)
            logits_out(0, 0)
            top_logit_waits(0)
            gram_out(0)
            top_logit(0, 0)
            scales_of(2, 2 + W_LOTS)
            link(nc.vector.tensor_copy(un_e[:].rearrange("p (n e) -> p n e", e=LOT),
                                       unscale[:, 2:2 + W_LOTS].unsqueeze(2).broadcast_to([P, W_LOTS, LOT])))
            dve.wait_ge(ex_ready, 1)
            top_gates(0, 0)
            identity_plus_eighth(0)
            gates_norm(0, 0)
            add_product(0, s2_done, s2, s3, 32, ALU.add, s2_ready)
            gates_scaled(0, 0)
            add_product(0, s1_done, s1, s2, 16, ALU.add, s1_ready)
            lot_low(0)
            add_product(0, s0_done, s0, s1, 8, ALU.subtract, s0_ready)

            def body(k, r):
                nxt, nn, nnn = exists(k + 1), exists(k + 2), exists(k + 3)
                low_tx(k)
                if nxt:
                    low_parts(k + 1, 1 - r)
                group(k, r, 0)
                err_out(k, r)
                if nnn:
                    stats_waits(k + 3)
                if nxt:
                    logits_out(k + 1, 1 - r)
                low_err(k, r)
                if nxt:
                    top_logit_waits(k + 1)
                    gram_out(k + 1)
                    top_logit(k + 1, 1 - r)
                if nnn:
                    stats_first(k + 3, 1 - r)
                    stats_second_waits(k + 3)
                if not past(k, 1):
                    lot_low(1)
                update(k)
                if nnn:
                    stats_second(k + 3, 1 - r)
                    guess_of(k + 3, 1 - r)
                group(k, r, 1)
                if past(k, 1):
                    gated(k - 1, 1 - r)
                else:
                    lot_low(2)
                low_state(k + 1)
                if nxt:
                    identity_plus_eighth(k + 1)
                group(k, r, 2)
                if nn:
                    normalize(k + 2, r)
                if nxt:
                    add_product(k + 1, s2_done, s2, s3, 32, ALU.add, s2_ready)
                    dve.wait_ge(ex_ready, k + 2)
                if not past(k, 1):
                    lot_low(3)
                group(k, r, 3)
                if nxt:
                    top_gates(k + 1, 1 - r)
                    add_product(k + 1, s1_done, s1, s2, 16, ALU.add, s1_ready)
                    gates_norm(k + 1, 1 - r)
                group(k, r, 4)
                if nxt:
                    add_product(k + 1, s0_done, s0, s1, 8, ALU.subtract, s0_ready)
                    gates_scaled(k + 1, 1 - r)
                group(k, r, 5)

            in_loop(dve, body)

            k, r = CHUNKS - 1, (CHUNKS - 1) % 2
            dve.wait_ge(z_step, ZS * (k + 1))
            dve.wait_ge(z_sum, 2 * k)
            nc.vector.tensor_tensor(zeo[:], zacc[:, r, 0, :], zacc[:, r, 1, :], ALU.add).then_inc(z_sum, 1)
            dve.wait_ge(part_sum, 3 * (k + 1))
            dve.wait_ge(z_sum, 2 * k + 1)
            nc.vector.tensor_tensor(z[:, r, :], zeo[:], parts[:], ALU.add).then_inc(z_sum, 1)
            dve.wait_ge(th_ready, k + 1)
            dve.wait_ge(z_sum, 2 * k + 2)
            nc.vector.scalar_tensor_tensor(out=silu2[:, r, :], in0=th[:, r, :], scalar=1.0, in1=z[:, r, :],
                                           op0=ALU.add, op1=ALU.mult).then_inc(silu_ready, 1)
            gated(k, r)
            dve.wait_ge(sg_ready, k + 1)
            dve.wait_ge(out_ready, k)
            nc.vector.tensor_tensor(x_all[:, k, :], sg[:, r, :], x_all[:, k, :], ALU.add).then_inc(out_ready, 1)

        @block.tensor
        def _(pe):
            def transposes(k, r):
                pe.wait_ge(xn_ready, k + 1)
                if past(k, 1):
                    pe.wait_ge(xl_ready, k)
                for h in range(HALVES):
                    last = nc.tensor.transpose(t_bank[:, h, 0:P], xn[:, r, h * P:(h + 1) * P], ident[:])
                last.then_inc(transposed, 1)

            def split_product(dst, r, hi, lo):
                for h in range(HALVES):
                    nc.tensor.matmul(dst, xt_hi[:, r, h, :], hi(h), start=(h == 0), stop=False)
                    nc.tensor.matmul(dst, xt_hi[:, r, h, :], lo(h), start=False, stop=False)
                for h in range(HALVES):
                    last = nc.tensor.matmul(dst, xt_lo[:, r, h, :], hi(h), start=False, stop=(h == HALVES - 1))
                return last

            def values_and_logits(k, r):
                pe.wait_ge(xh_ready, k + 1)
                pe.wait_ge(xl_ready, k + 1)
                if past(k, 1):
                    pe.wait_ge(v_ready, k)
                split_product(vr_bank[:, 0:VR], r, lambda h: vr_hi[:, h, :], lambda h: vr_lo[:, h, :]).then_inc(vr_done, 1)

            def gram(k):
                pe.wait_ge(xt_ready, k + 1)
                for h in range(HALVES):
                    last = nc.tensor.matmul(inv_bank[:, 0, :], xt[:, h, :], xt[:, h, :], start=(h == 0),
                                            stop=(h == HALVES - 1))
                last.then_inc(gram_done, 1)

            def squares(k):
                pe.wait_ge(n1_ready, k + 1)
                nc.tensor.matmul(inv_bank[:, 0, 0:P - 16], n1t[:], n1[:, 0:P - 16], start=True, stop=True)
                nc.tensor.matmul(inv_bank[:, 1, 16:P], n1[:], n1t[:, 16:P], start=True, stop=True).then_inc(p2_done, 1)

            def fourths(k):
                pe.wait_ge(n2_ready, k + 1)
                nc.tensor.matmul(inv_bank[:, 0, 0:P - 32], n2t[:], n2[:, 0:P - 32], start=True, stop=True)
                nc.tensor.matmul(inv_bank[:, 1, 64:P], n2[:], n2t[:, 64:P], start=True, stop=True).then_inc(p4_done, 1)

            def eighth(k):
                pe.wait_ge(n4_ready, k + 1)
                nc.tensor.matmul(inv_bank[:, 0, 64:P], n4[:], n4t[:, 64:P], start=True, stop=True).then_inc(p8_done, 1)

            def product(k, ready, left, right, first, done):
                pe.wait_ge(ready, k + 1)
                nc.tensor.matmul(inv_bank[:, 0, first:P], left[:], right[:, first:P], start=True,
                                 stop=True).then_inc(done, 1)

            def tx(k, r):
                pe.wait_ge(s0_ready, k + 1)
                if past(k, 1):
                    pe.wait_ge(state_ready, k)
                for h in range(HALVES):
                    nc.tensor.matmul(mem_bank[:, h * P:(h + 1) * P], xn[:, r, h * P:(h + 1) * P], s0[:],
                                     start=True, stop=True)
                nc.tensor.matmul(mem_bank[:, D:D + 1], s0[:], ones[:], start=True, stop=True).then_inc(tx_done, 1)

            def errors(k):
                pe.wait_ge(tx_ready, k + 1)
                pe.wait_ge(tx_low, k + 1)
                pe.wait_ge(state_high, k + 1)
                pe.wait_ge(state_low, k + 1)
                dst = mem_bank[:, 0:D]
                for h in range(HALVES):
                    nc.tensor.matmul(dst, tx_hi[:, h, :], state_hi[:, h, :], start=(h == 0), stop=False)
                    nc.tensor.matmul(dst, tx_hi[:, h, :], state_lo[:, h, :], start=False, stop=False)
                    last = nc.tensor.matmul(dst, tx_lo[:, h, :], state_hi[:, h, :], start=False,
                                            stop=(h == HALVES - 1))
                last.then_inc(err_done, 1)

            def gradient(k):
                pe.wait_ge(rows_high, k + 1)
                pe.wait_ge(rows_low, k + 1)
                pe.wait_ge(err_high, k + 1)
                pe.wait_ge(err_low, k + 1)
                for h in range(HALVES):
                    dst, rows = mem_bank[:, h * D:(h + 1) * D], slice(h * P, (h + 1) * P)
                    nc.tensor.matmul(dst, xn_hi[:, rows], err_hi[:], start=True, stop=False)
                    nc.tensor.matmul(dst, xn_hi[:, rows], err_lo[:], start=False, stop=False)
                    last = nc.tensor.matmul(dst, xn_lo[:, rows], err_hi[:], start=False, stop=True)
                last.then_inc(grad_done, 1)

            def experts(k, r, g):
                bank = g % EXPERT_BANKS
                if isinstance(k, int) and k == 0 and g < EXPERT_BANKS:
                    pass
                elif (g - EXPERT_BANKS) % GROUPS in ACT_GROUPS:
                    n = ACT_GROUPS.index((g - EXPERT_BANKS) % GROUPS)
                    pe.wait_ge(part_step, PS * (k if g >= EXPERT_BANKS else k - 1) + 2 * (n + 1))
                else:
                    n = DVE_GROUPS.index((g - EXPERT_BANKS) % GROUPS)
                    pe.wait_ge(z_step, ZS * (k if g >= EXPERT_BANKS else k - 1) + 2 * (n + 1))
                if isinstance(k, int) and k == 0:
                    pe.wait_ge(hi_ready, 3 + 2 * g // LOT)
                    pe.wait_ge(lo_ready, 3 + 2 * g // LOT)
                split_product(e_bank[bank][:], r, lambda h: w_hi[:, h, 2 * g:2 * g + 2, :],
                              lambda h: w_lo[:, h, 2 * g:2 * g + 2, :]).then_inc(group_done[bank], 1)

            pe.wait_ge(const_ready, 15)
            transposes(0, 0)
            pe.wait_ge(hi_ready, 2)
            pe.wait_ge(lo_ready, 2)
            values_and_logits(0, 0)
            gram(0)
            squares(0)
            fourths(0)
            eighth(0)
            product(0, s3_ready, n4, s3, 32, s2_done)
            product(0, s2_ready, n2, s2, 16, s1_done)
            product(0, s1_ready, n1, s1, 8, s0_done)

            def body(k, r):
                more = exists(k + 1)
                if more:
                    transposes(k + 1, 1 - r)
                tx(k, r)
                experts(k, r, 0)
                errors(k)
                if more:
                    values_and_logits(k + 1, 1 - r)
                    gram(k + 1)
                experts(k, r, 1)
                gradient(k)
                if more:
                    squares(k + 1)
                experts(k, r, 2)
                if more:
                    fourths(k + 1)
                experts(k, r, 3)
                if more:
                    eighth(k + 1)
                experts(k, r, 4)
                if more:
                    product(k + 1, s3_ready, n4, s3, 32, s2_done)
                experts(k, r, 5)
                if more:
                    product(k + 1, s2_ready, n2, s2, 16, s1_done)
                experts(k, r, 6)
                if more:
                    product(k + 1, s1_ready, n1, s1, 8, s0_done)
                experts(k, r, 7)

            in_loop(pe, body)


def kernel(L0_attn_x, L0_attn_W0, L0_attn_Wkv, L0_attn_bkv, L0_attn_eta, L0_ffn_router_w, L0_ffn_router_b,
           L0_ffn_expert_w):
    import numpy as np
    import concourse.bacc as bacc
    from concourse.bass_utils import run_bass_kernel_spmd

    def halves(w):
        return np.ascontiguousarray(np.asarray(w).reshape(HALVES, P, -1).transpose(1, 0, 2))

    x = np.asarray(L0_attn_x)
    wkv, bkv = np.asarray(L0_attn_Wkv), np.asarray(L0_attn_bkv)
    rows = x.transpose(1, 0, 2).reshape(CHUNKS, P, D).transpose(1, 0, 2)
    arrays = {
        "x_rows": np.ascontiguousarray(rows),
        "w0_t": halves(np.asarray(L0_attn_W0).T),
        "wv_router_t": halves(np.concatenate([wkv[D:].T, np.asarray(L0_ffn_router_w).T], axis=1)),
        "experts": np.ascontiguousarray(
            np.asarray(L0_ffn_expert_w).reshape(EXPERTS, HALVES, P, D).transpose(2, 1, 0, 3)),
        "bias_v": np.ascontiguousarray(bkv[D:].reshape(1, D)),
        "router_b": np.ascontiguousarray(np.asarray(L0_ffn_router_b).reshape(1, EXPERTS)),
        "eta_in": np.ascontiguousarray(np.asarray(L0_attn_eta).reshape(1, 1)),
    }
    nc = bacc.Bacc("TRN2", target_bir_lowering=False, num_devices=1)
    args = [nc.dram_tensor(n, a.shape, mybir.dt.from_np(a.dtype), kind="ExternalInput").ap()
            for n, a in arrays.items()]
    out = nc.dram_tensor("out_rows", (P, CHUNKS, D), FP32, kind="ExternalOutput").ap()
    program(nc, *args, out)
    result = run_bass_kernel_spmd(nc, [arrays], core_ids=[0])
    got = np.asarray(result.results[0]["out_rows"])
    return np.ascontiguousarray(got.transpose(1, 0, 2).reshape(STEPS, BATCH, D).transpose(1, 0, 2))
```

```python
import concourse.bass as bass
from concourse import mybir
from contextlib import ExitStack

FP32 = mybir.dt.float32
FP16 = mybir.dt.float16
FP32R = mybir.dt.float32r
INT32 = mybir.dt.int32
ALU = mybir.AluOpType
ACT = mybir.ActivationFunctionType
ALL_ADD = bass.bass_isa.ReduceOp.add

P = 128
BATCH, STEPS, D = 8, 1024, 256
CHUNK_STEPS = P // BATCH
CHUNKS = STEPS // CHUNK_STEPS
TWO, FOUR, EIGHT = 2 * BATCH, 4 * BATCH, 8 * BATCH
HALVES = D // P
EXPERTS, TOP_K = 16, 6
GROUPS = EXPERTS // 2
EXPERT_BANKS = 4
LN_EPS, EPS = 1e-5, 1e-10
VR = D + EXPERTS
X_SCALE = 256.0
W_TOP = 16384.0
W_LOTS = 8
FIRST_LOTS = 2
LOT = EXPERTS // W_LOTS
POOL_LOTS = (4, 5, 7)
DVE_LOTS = tuple(n for n in range(W_LOTS) if n not in POOL_LOTS)
HEAD = 3
FIRST, LAST = 2, 4
ACT_GROUPS = (1, 5)
DVE_GROUPS = tuple(g for g in range(GROUPS) if g not in ACT_GROUPS)
ZS = 2 * len(DVE_GROUPS)
PS = 2 * len(ACT_GROUPS)
MAGIC = 0x5F3759DF
EXPONENT = 0x7F800000


def program(nc, x_in, w0t_in, wvr_in, expert_in, b_in, rb_in, eta_in, out):
    ctx = ExitStack()
    with ctx:
        def sb(name, shape, dt=FP32):
            return ctx.enter_context(nc.sbuf_tensor(name, shape, dt))

        def pb(name, shape):
            return ctx.enter_context(nc.psum_tensor(name, shape, FP32))

        def sem(name):
            return ctx.enter_context(nc.semaphore(name))

        x_all = sb("x_all", [P, CHUNKS, D])
        w_raw = sb("w_raw", [P, HALVES, EXPERTS, D])
        w_hi = sb("w_hi", [P, HALVES, EXPERTS, D], FP16)
        w_lo = sb("w_lo", [P, HALVES, EXPERTS, D], FP16)
        vr_raw = sb("vr_raw", [P, HALVES, VR])
        vr_hi = sb("vr_hi", [P, HALVES, VR], FP16)
        vr_lo = sb("vr_lo", [P, HALVES, VR], FP16)
        state = sb("state", [P, HALVES, D])
        b_row = sb("b_row", [P, D])
        rb_row = sb("rb_row", [P, EXPERTS])
        eta = sb("eta", [P, 1])
        neg_c = sb("neg_c", [P, 1])
        ident = sb("ident", [P, P])
        lower = sb("lower", [P, P])
        upper = sb("upper", [P, P])
        squares_p = sb("squares_p", [P, 2 + W_LOTS])
        squares_all = sb("squares_all", [P, 2 + W_LOTS])
        clamped = sb("clamped", [P, 2 + W_LOTS])
        halved = sb("halved", [P, 2 + W_LOTS], INT32)
        shifted = sb("shifted", [P, 2 + W_LOTS], INT32)
        c_pos = sb("c_pos", [P, 1])
        power = sb("power", [P, 2 + W_LOTS])
        rpower = sb("rpower", [P, 2 + W_LOTS])
        scale = sb("scale", [P, 2 + W_LOTS])
        unscale = sb("unscale", [P, 2 + W_LOTS])
        un_e = sb("un_e", [P, EXPERTS])
        q = sb("q", [P, 1])
        half_unq = sb("half_unq", [P, 1])

        stats = sb("stats", [P, 2, 6])
        mv = sb("mv", [P, 2, 2])
        vare = sb("vare", [P, 2, 1])
        nvh = sb("nvh", [P, 2, 1])
        half_bits = sb("half_bits", [P, 2, 1], INT32)
        rs = [sb(f"rs{n}", [P, 2, 1]) for n in range(4)]
        nt_a = sb("nt_a", [P, 2, 3])
        nt_b = sb("nt_b", [P, 2, 3])
        nt_c = sb("nt_c", [P, 2, 3])
        neg_half = sb("neg_half", [P, 1])
        three_halves = sb("three_halves", [P, 1])
        xn = sb("xn", [P, 2, D])
        xt = sb("xt", [P, HALVES, P])
        xt_hi = sb("xt_hi", [P, 2, HALVES, P], FP16)
        xt_lo = sb("xt_lo", [P, 2, HALVES, P], FP16)
        n1 = sb("n1", [P, P])
        n1t = sb("n1t", [P, P])
        n2 = sb("n2", [P, P])
        n2t = sb("n2t", [P, P])
        n4 = sb("n4", [P, P])
        half8 = sb("half8", [P, P])
        s0 = sb("s0", [P, P])
        xr_hi = sb("xr_hi", [P, HALVES, P], FP32R)
        xr_lo = sb("xr_lo", [P, HALVES, P], FP32R)
        resid = sb("resid", [P, D])
        resid_hi = sb("resid_hi", [P, D], FP32R)
        resid_lo = sb("resid_lo", [P, D], FP32R)
        s0_hi = sb("s0_hi", [P, P], FP32R)
        s0_lo = sb("s0_lo", [P, P], FP32R)
        xn_hi = sb("xn_hi", [P, D], FP32R)
        xn_lo = sb("xn_lo", [P, D], FP32R)
        err_hi = sb("err_hi", [P, D], FP32R)
        err_lo = sb("err_lo", [P, D], FP32R)
        state_hi = sb("state_hi", [P, HALVES, D], FP32R)
        state_lo = sb("state_lo", [P, HALVES, D], FP32R)
        err = sb("err", [P, 2, D])
        v = sb("v", [P, 2, D])
        y = sb("y", [P, 2, D])
        logit = sb("logit", [P, 2, EXPERTS])
        top_l = sb("top_l", [P, 2, 8])
        neg_max = sb("neg_max", [P, 2, 1])
        ex = sb("ex", [P, 2, EXPERTS + 2])
        ex_sum = sb("ex_sum", [P, 2, 1])
        top_e = sb("top_e", [P, 2, 8])
        rest = sb("rest", [P, 2, EXPERTS + 2])
        ex_eps = sb("ex_eps", [P, 2, 1])
        sel = sb("sel", [P, 2, EXPERTS])
        sel_sum = sb("sel_sum", [P, 2, 1])
        denom = sb("denom", [P, 2, 1])
        rdenom = sb("rdenom", [P, 2, 1])
        eps_term = sb("eps_term", [P, 2, 1])
        acc = sb("acc", [P, 2, 1])
        racc = sb("racc", [P, 2, 1])
        factor = sb("factor", [P, 2, 1])
        gate = sb("gate", [P, 2, EXPERTS])
        zacc = sb("zacc", [P, 2, 2, D])
        part = sb("part", [P, 2, PS, D])
        psum01 = sb("psum01", [P, D])
        psum23 = sb("psum23", [P, D])
        parts = sb("parts", [P, D])
        zeo = sb("zeo", [P, D])
        z = sb("z", [P, 2, D])
        th = sb("th", [P, 2, D])
        zt = sb("zt", [P, D])
        silu2 = sb("silu2", [P, 2, D])
        sg = sb("sg", [P, 2, D])

        t_bank = pb("t_bank", [P, HALVES, D])
        vr_bank = pb("vr_bank", [P, 512])
        inv_bank = pb("inv_bank", [P, 4, P])
        mem_bank = pb("mem_bank", [P, 512])
        e_bank = [pb(f"e_bank{n}", [P, 512]) for n in range(EXPERT_BANKS)]

        x_loaded = sem("x_loaded")
        small_loaded = sem("small_loaded")
        vr_loaded = sem("vr_loaded")
        w_loaded = [sem(f"w_loaded{n}") for n in range(W_LOTS)]
        stored = sem("stored")
        const_ready = sem("const_ready")
        mask_scaled = sem("mask_scaled")
        squares_ready = sem("squares_ready")
        all_ready = sem("all_ready")
        scale_ready = sem("scale_ready")
        pool_low_ready = sem("pool_low_ready")
        hi_ready = sem("hi_ready")
        lo_ready = sem("lo_ready")
        setup_step = sem("setup_step")
        setup_pool = sem("setup_pool")
        lot_is_scaled = sem("lot_is_scaled")
        state_ready = sem("state_ready")
        state_high = sem("state_high")
        state_low = sem("state_low")
        rows_high = sem("rows_high")
        rows_low = sem("rows_low")
        err_high = sem("err_high")
        err_low = sem("err_low")
        xr_high = sem("xr_high")
        xr_low = sem("xr_low")
        stat_step = sem("stat_step")
        newton = sem("newton")
        xn_ready = sem("xn_ready")
        transposed = sem("transposed")
        xh_ready = sem("xh_ready")
        xt_ready = sem("xt_ready")
        xl_ready = sem("xl_ready")
        vr_done = sem("vr_done")
        v_ready = sem("v_ready")
        route = sem("route")
        first_gates_ready = sem("first_gates_ready")
        ex_ready = sem("ex_ready")
        gram_done = sem("gram_done")
        n1_ready = sem("n1_ready")
        first_ready = sem("first_ready")
        p2_done = sem("p2_done")
        n2_ready = sem("n2_ready")
        p4_done = sem("p4_done")
        n4_ready = sem("n4_ready")
        s2_ready = sem("s2_ready")
        prod4_done = sem("prod4_done")
        s4_ready = sem("s4_ready")
        half8_done = sem("half8_done")
        half8_ready = sem("half8_ready")
        s0_done = sem("s0_done")
        s0_ready = sem("s0_ready")
        mem_done = sem("mem_done")
        resid_ready = sem("resid_ready")
        resid_high = sem("resid_high")
        resid_low = sem("resid_low")
        s0_high = sem("s0_high")
        s0_low = sem("s0_low")
        err_done = sem("err_done")
        err_ready = sem("err_ready")
        grad_done = sem("grad_done")
        group_done = [sem(f"group_done{n}") for n in range(EXPERT_BANKS)]
        z_step = sem("z_step")
        part_step = sem("part_step")
        part_sum = sem("part_sum")
        z_sum = sem("z_sum")
        y_ready = sem("y_ready")
        th_ready = sem("th_ready")
        zt_ready = sem("zt_ready")
        silu_ready = sem("silu_ready")
        sg_ready = sem("sg_ready")
        out_ready = sem("out_ready")
        ROUTE, STAT, NEWTON = 15, 5, 13

        def past(k, n):
            return not isinstance(k, int) or k >= n

        def in_loop(eng, body):
            for k in range(FIRST):
                body(k, k % 2)
            with eng.Fori(0, (CHUNKS - FIRST - LAST) // 2) as pair:
                for r in range(2):
                    body(2 * pair + (FIRST + r), r)
            for k in range(CHUNKS - LAST, CHUNKS):
                body(k, k % 2)

        def exists(k):
            return not isinstance(k, int) or k < CHUNKS

        def load_lot(eng, n):
            lot = slice(n * LOT, (n + 1) * LOT)
            eng.dma_start(w_raw[:, :, lot, :], expert_in[:, :, lot, :]).then_inc(w_loaded[n], 16)

        block = ctx.enter_context(nc.Block())

        @block.sync
        def _(sp):
            sp.dma_start(x_all[:, 0:HEAD, :], x_in[:, 0:HEAD, :]).then_inc(x_loaded, 16)
            sp.wait_ge(vr_loaded, 16)
            for n in range(FIRST_LOTS, W_LOTS):
                load_lot(sp, n)
            with sp.Fori(HEAD, CHUNKS) as k:
                sp.wait_ge(x_loaded, 16 * (k - (HEAD - 1)))
                sp.dma_start(x_all[:, k, :], x_in[:, k, :]).then_inc(x_loaded, 16)
            with sp.Fori(0, CHUNKS) as k:
                sp.wait_ge(out_ready, k + 1)
                sp.dma_start(out[:, k, :], x_all[:, k, :]).then_inc(stored, 16)
            sp.wait_ge(stored, 16 * CHUNKS)

        @block.gpsimd
        def _(pool):
            nc.gpsimd.memset(ident[:], 0.0).then_inc(setup_pool, 1)
            nc.gpsimd.memset(lower[:], 1.0).then_inc(setup_pool, 1)
            nc.gpsimd.memset(upper[:], 1.0).then_inc(setup_pool, 1)
            pool.wait_ge(setup_pool, 3)
            nc.gpsimd.affine_select(out=ident[:], in_=ident[:], compare_op=ALU.not_equal, fill=1.0, base=0,
                                    pattern=[[-1, P]], channel_multiplier=1).then_inc(const_ready, 1)
            low3 = lower[:].rearrange("p (j r) -> p j r", r=BATCH)
            upp3 = upper[:].rearrange("p (j r) -> p j r", r=BATCH)
            nc.gpsimd.affine_select(out=low3, in_=low3, compare_op=ALU.is_ge, fill=0.0, base=-BATCH,
                                    pattern=[[-BATCH, CHUNK_STEPS], [0, BATCH]],
                                    channel_multiplier=1).then_inc(const_ready, 1)
            nc.gpsimd.affine_select(out=upp3, in_=upp3, compare_op=ALU.is_ge, fill=0.0, base=-1,
                                    pattern=[[BATCH, CHUNK_STEPS], [0, BATCH]],
                                    channel_multiplier=-1).then_inc(const_ready, 1)
            nc.gpsimd.memset(neg_half[:], -0.5).then_inc(const_ready, 1)
            nc.gpsimd.memset(three_halves[:], 1.5).then_inc(const_ready, 1)
            nc.gpsimd.memset(ex[:], -1.0).then_inc(const_ready, 1)
            for t in (n2, n2t, n4, half8):
                nc.gpsimd.memset(t[:], 0.0).then_inc(const_ready, 1)
            def all_squares(first, last):
                pool.wait_ge(squares_ready, last)
                nc.gpsimd.partition_all_reduce(squares_all[:, first:last], squares_p[:, first:last], P,
                                               ALL_ADD).then_inc(all_ready, 1)

            def newton_steps(k, r):
                pool.wait_ge(stat_step, STAT * (k + 1))
                base = NEWTON * k
                nc.gpsimd.tensor_tensor(nvh[:, r, :], vare[:, r, :], neg_half[:], ALU.mult).then_inc(newton, 1)
                for n in range(3):
                    if isinstance(k, int) and k == 0 and n == 2:
                        all_squares(0, 2)
                    guess, a, b, c = rs[n][:, r, :], nt_a[:, r, n:n + 1], nt_b[:, r, n:n + 1], nt_c[:, r, n:n + 1]
                    nc.gpsimd.tensor_tensor(a, guess, guess, ALU.mult).then_inc(newton, 1)
                    pool.wait_ge(newton, base + (4 * n + 2))
                    nc.gpsimd.tensor_tensor(b, a, nvh[:, r, :], ALU.mult).then_inc(newton, 1)
                    pool.wait_ge(newton, base + (4 * n + 3))
                    nc.gpsimd.tensor_tensor(c, b, three_halves[:], ALU.add).then_inc(newton, 1)
                    pool.wait_ge(newton, base + (4 * n + 4))
                    if n == 2 and past(k, 2):
                        pool.wait_ge(xn_ready, k - 1)
                    nc.gpsimd.tensor_tensor(rs[n + 1][:, r, :], guess, c, ALU.mult).then_inc(newton, 1)
                    if n < 2:
                        pool.wait_ge(newton, base + (4 * n + 5))

            pool.wait_ge(const_ready, 6)
            newton_steps(0, 0)
            def z_total(k, r):
                pool.wait_ge(z_step, ZS * (k + 1))
                nc.gpsimd.tensor_tensor(zeo[:], zacc[:, r, 0, :], zacc[:, r, 1, :], ALU.add).then_inc(z_sum, 1)
                pool.wait_ge(part_sum, 3 * (k + 1))
                pool.wait_ge(z_sum, 2 * k + 1)
                if past(k, 2):
                    pool.wait_ge(th_ready, k - 1)
                nc.gpsimd.tensor_tensor(z[:, r, :], zeo[:], parts[:], ALU.add).then_inc(z_sum, 1)

            def silu_of(k, r):
                pool.wait_ge(th_ready, k + 1)
                nc.gpsimd.tensor_tensor(zt[:], z[:, r, :], th[:, r, :], ALU.mult).then_inc(zt_ready, 1)
                pool.wait_ge(zt_ready, k + 1)
                if past(k, 2):
                    pool.wait_ge(sg_ready, k - 1)
                nc.gpsimd.tensor_tensor(silu2[:, r, :], z[:, r, :], zt[:], ALU.add).then_inc(silu_ready, 1)

            def low_xr(k):
                pool.wait_ge(xr_high, k + 1)
                if past(k, 1):
                    pool.wait_ge(mem_done, k)
                nc.gpsimd.tensor_tensor(xr_lo[:], xt[:], xr_hi[:].bitcast(FP32), ALU.subtract).then_inc(xr_low, 1)

            def low_inverse(k):
                pool.wait_ge(s0_high, k + 1)
                if past(k, 1):
                    pool.wait_ge(err_done, k)
                nc.gpsimd.tensor_tensor(s0_lo[:], s0[:], s0_hi[:].bitcast(FP32), ALU.subtract).then_inc(s0_low, 1)

            def low_rows(k, r):
                pool.wait_ge(rows_high, k + 1)
                nc.gpsimd.tensor_tensor(xn_lo[:], xn[:, r, :], xn_hi[:].bitcast(FP32),
                                        ALU.subtract).then_inc(rows_low, 1)

            def low_lot(n):
                pool.wait_ge(lot_is_scaled, n + 1)
                lot = slice(POOL_LOTS[n] * LOT, (POOL_LOTS[n] + 1) * LOT)
                nc.gpsimd.tensor_tensor(w_lo[:, :, lot, :].rearrange("p h e d -> p h (e d)"),
                                        w_raw[:, :, lot, :].rearrange("p h e d -> p h (e d)"),
                                        w_hi[:, :, lot, :].rearrange("p h e d -> p h (e d)"),
                                        ALU.subtract).then_inc(pool_low_ready, 1)

            def result(k, r):
                pool.wait_ge(sg_ready, k + 1)
                nc.gpsimd.tensor_tensor(x_all[:, k, :], sg[:, r, :], x_all[:, k, :],
                                        ALU.add).then_inc(out_ready, 1)

            def body(k, r):
                low_inverse(k)
                if not past(k, 1):
                    all_squares(8, 10)
                low_rows(k, r)
                if past(k, 1):
                    z_total(k - 1, 1 - r)
                    silu_of(k - 1, 1 - r)
                pool.wait_ge(err_ready, k + 1)
                pool.wait_ge(v_ready, k + 1)
                if past(k, 2):
                    pool.wait_ge(sg_ready, k - 1)
                nc.gpsimd.tensor_tensor(y[:, r, :], err[:, r, :], v[:, r, :], ALU.add).then_inc(y_ready, 1)
                if exists(k + 1):
                    low_xr(k + 1)
                if not past(k, 1):
                    low_lot(0)
                    low_lot(1)
                pool.wait_ge(part_step, PS * k + 2)
                if past(k, 1):
                    pool.wait_ge(part_sum, 3 * k)
                nc.gpsimd.tensor_tensor(psum01[:], part[:, r, 0, :], part[:, r, 1, :],
                                        ALU.add).then_inc(part_sum, 1)
                if past(k, 1):
                    result(k - 1, 1 - r)
                else:
                    low_lot(2)
                if exists(k + 3):
                    newton_steps(k + 3, 1 - r)
                pool.wait_ge(part_step, PS * k + 4)
                nc.gpsimd.tensor_tensor(psum23[:], part[:, r, 2, :], part[:, r, 3, :],
                                        ALU.add).then_inc(part_sum, 1)
                pool.wait_ge(part_sum, 3 * k + 2)
                if past(k, 1):
                    pool.wait_ge(z_sum, 2 * k)
                nc.gpsimd.tensor_tensor(parts[:], psum01[:], psum23[:], ALU.add).then_inc(part_sum, 1)

            all_squares(2, 4)
            newton_steps(1, 1)
            low_xr(0)
            all_squares(4, 6)
            newton_steps(2, 0)
            all_squares(6, 8)
            in_loop(pool, body)

        @block.scalar
        def _(act):
            act.dma_start(vr_raw[:], wvr_in).then_inc(vr_loaded, 16)
            act.dma_start(state[:], w0t_in).then_inc(small_loaded, 16)
            act.dma_start(b_row[:], b_in.broadcast_to([P, D])).then_inc(small_loaded, 16)
            act.dma_start(rb_row[:], rb_in.broadcast_to([P, EXPERTS])).then_inc(small_loaded, 16)
            act.dma_start(eta[:], eta_in.broadcast_to([P, 1])).then_inc(small_loaded, 16)
            for n in range(FIRST_LOTS):
                load_lot(act, n)

            def high_parts(k, r):
                act.wait_ge(transposed, k + 1)
                if past(k, 2):
                    act.wait_ge(group_done[EXPERT_BANKS - 1], 2 * (k - 1))
                nc.scalar.activation(xt_hi[:, r, :, :], t_bank[:, :, 0:P], ACT.Copy,
                                     scale=X_SCALE).then_inc(xh_ready, 1)

            def transposed_out(k):
                if past(k, 1):
                    act.wait_ge(xr_low, k)
                nc.scalar.activation(xt[:], t_bank[:, :, 0:P], ACT.Copy).then_inc(xt_ready, 1)

            def high_xr(k):
                if past(k, 1):
                    act.wait_ge(mem_done, k)
                    act.wait_ge(xr_low, k)
                act.wait_ge(xt_ready, k + 1)
                nc.scalar.activation(xr_hi[:], xt[:], ACT.Copy).then_inc(xr_high, 1)

            def high_rows(k, r):
                if past(k, 1):
                    act.wait_ge(grad_done, k)
                    act.wait_ge(rows_low, k)
                act.wait_ge(xn_ready, k + 1)
                nc.scalar.activation(xn_hi[:], xn[:, r, :], ACT.Copy).then_inc(rows_high, 1)

            def high_inverse(k):
                act.wait_ge(s0_ready, k + 1)
                if past(k, 1):
                    act.wait_ge(s0_low, k)
                    act.wait_ge(err_done, k)
                nc.scalar.activation(s0_hi[:], s0[:], ACT.Copy).then_inc(s0_high, 1)

            def high_residual(k):
                act.wait_ge(resid_ready, k + 1)
                if past(k, 1):
                    act.wait_ge(err_done, k)
                nc.scalar.activation(resid_hi[:], resid[:], ACT.Copy).then_inc(resid_high, 1)

            def err_out(k, r):
                act.wait_ge(err_done, k + 1)
                if past(k, 2):
                    act.wait_ge(y_ready, k - 1)
                nc.scalar.activation(err[:, r, :], mem_bank[:, D:2 * D], ACT.Copy).then_inc(err_ready, 1)
                if past(k, 1):
                    act.wait_ge(err_low, k)
                nc.scalar.activation(err_hi[:], mem_bank[:, D:2 * D], ACT.Copy).then_inc(err_high, 1)

            def high_state(k):
                act.wait_ge(state_ready, k + 1)
                nc.scalar.activation(state_hi[:], state[:], ACT.Copy).then_inc(state_high, 1)

            def group(k, r, n):
                g = ACT_GROUPS[n]
                bank = g % EXPERT_BANKS
                act.wait_ge(group_done[bank], 2 * k + (g // EXPERT_BANKS + 1))
                if n == 0:
                    act.wait_ge(route, ROUTE * (k + 1))
                    if not past(k, 1):
                        act.wait_ge(first_gates_ready, 1)
                    if past(k, 2):
                        act.wait_ge(part_sum, 3 * (k - 1))
                for j in range(2):
                    e = 2 * g + j
                    nc.scalar.activation(part[:, r, 2 * n + j, :], e_bank[bank][:, j * D:(j + 1) * D], ACT.Copy,
                                         scale=gate[:, r, e:e + 1]).then_inc(part_step, 1)

            def squares(k):
                act.wait_ge(p2_done, k + 1)
                nc.scalar.activation(n2[:, 0:P - TWO], inv_bank[:, 0, 0:P - TWO], ACT.Copy)
                nc.scalar.activation(n2t[:, TWO:P], inv_bank[:, 1, TWO:P], ACT.Copy).then_inc(n2_ready, 1)

            def fourths(k):
                act.wait_ge(p4_done, k + 1)
                nc.scalar.activation(n4[:, 0:P - FOUR], inv_bank[:, 0, 0:P - FOUR], ACT.Copy).then_inc(n4_ready, 1)

            def half_of_8(k):
                act.wait_ge(half8_done, k + 1)
                nc.scalar.activation(half8[0:P - FOUR, EIGHT:P], inv_bank[0:P - FOUR, 3, EIGHT:P], ACT.Copy).then_inc(half8_ready, 1)

            def exponent(k, r):
                act.wait_ge(route, ROUTE * k + 3)
                nc.scalar.activation(ex[:, r, 0:EXPERTS], logit[:, r, :], ACT.Exp, bias=neg_max[:, r, :],
                                     accum_out=ex_sum[:, r, :]).then_inc(ex_ready, 1)

            def tanh_of(k, r):
                act.wait_ge(z_sum, 2 * (k + 1))
                if past(k, 2):
                    act.wait_ge(silu_ready, k - 1)
                nc.scalar.activation(th[:, r, :], z[:, r, :], ACT.Tanh, scale=0.5).then_inc(th_ready, 1)

            def lot_squares(n):
                act.wait_ge(w_loaded[n], 16)
                lot = slice(n * LOT, (n + 1) * LOT)
                nc.scalar.activation(w_lo[:, :, lot, :].rearrange("p h e d -> p h (e d)"),
                                     w_raw[:, :, lot, :].rearrange("p h e d -> p h (e d)"), ACT.Square,
                                     accum_out=squares_p[:, 2 + n:3 + n]).then_inc(squares_ready, 1)

            def lot_high(n):
                act.wait_ge(scale_ready, min(2 + n // 2, 4))
                lot = slice(n * LOT, (n + 1) * LOT)
                nc.scalar.activation(w_hi[:, :, lot, :].rearrange("p h e d -> p h (e d)"),
                                     w_raw[:, :, lot, :].rearrange("p h e d -> p h (e d)"), ACT.Copy,
                                     scale=scale[:, 2 + n:3 + n]).then_inc(hi_ready, 1)

            def lot_scaled(n):
                act.wait_ge(scale_ready, min(2 + n // 2, 4))
                act.wait_ge(hi_ready, 3 + n)
                lot = slice(n * LOT, (n + 1) * LOT)
                flat = w_raw[:, :, lot, :].rearrange("p h e d -> p h (e d)")
                nc.scalar.activation(flat, flat, ACT.Copy, scale=scale[:, 2 + n:3 + n]).then_inc(lot_is_scaled, 1)

            act.wait_ge(vr_loaded, 16)
            nc.scalar.activation(vr_lo[:, :, 0:D], vr_raw[:, :, 0:D], ACT.Square,
                                 accum_out=squares_p[:, 0:1]).then_inc(squares_ready, 1)
            nc.scalar.activation(vr_lo[:, :, D:VR], vr_raw[:, :, D:VR], ACT.Square,
                                 accum_out=squares_p[:, 1:2]).then_inc(squares_ready, 1)
            act.wait_ge(scale_ready, 1)
            nc.scalar.activation(vr_hi[:, :, 0:D], vr_raw[:, :, 0:D], ACT.Copy, scale=scale[:, 0:1]).then_inc(hi_ready, 1)
            nc.scalar.activation(vr_hi[:, :, D:VR], vr_raw[:, :, D:VR], ACT.Copy,
                                 scale=scale[:, 1:2]).then_inc(hi_ready, 1)
            high_parts(0, 0)
            transposed_out(0)
            high_xr(0)
            for n in range(4):
                lot_squares(n)
            act.wait_ge(const_ready, 10)
            squares(0)
            lot_squares(4)
            fourths(0)
            exponent(0, 0)
            lot_high(0)
            half_of_8(0)
            lot_high(1)
            lot_squares(5)

            def body(k, r):
                if exists(k + 1):
                    high_parts(k + 1, 1 - r)
                if exists(k + 1):
                    transposed_out(k + 1)
                if not past(k, 1):
                    lot_squares(6)
                high_inverse(k)
                high_residual(k)
                if not past(k, 1):
                    lot_squares(7)
                high_rows(k, r)
                if exists(k + 1):
                    high_xr(k + 1)
                if not past(k, 1):
                    lot_high(2)
                err_out(k, r)
                if past(k, 1):
                    tanh_of(k - 1, 1 - r)
                    group(k, r, 0)
                if exists(k + 1):
                    squares(k + 1)
                if past(k, 1):
                    if exists(k + 1):
                        exponent(k + 1, 1 - r)
                    high_state(k)
                    if exists(k + 1):
                        fourths(k + 1)
                else:
                    lot_high(3)
                    lot_high(4)
                    lot_scaled(4)
                    lot_high(5)
                    lot_scaled(5)
                    lot_high(6)
                    fourths(k + 1)
                    group(k, r, 0)
                    exponent(k + 1, 1 - r)
                    high_state(k)
                    lot_high(7)
                    lot_scaled(7)
                group(k, r, 1)
                if exists(k + 1):
                    half_of_8(k + 1)

            in_loop(act, body)
            last = CHUNKS - 1
            tanh_of(last, last % 2)

        @block.vector
        def _(dve):
            def stats_waits(k):
                dve.wait_ge(x_loaded, 16 if isinstance(k, int) and k < HEAD else 16 * (k - (HEAD - 2)))

            def stats_first(k, r):
                nc.vector.bn_stats(stats[:, r, :], x_all[:, k, :]).then_inc(stat_step, 1)

            def stats_second_waits(k):
                if past(k, 2):
                    dve.wait_ge(xn_ready, k - 1)
                dve.wait_ge(stat_step, STAT * k + 1)

            def stats_second(k, r):
                nc.vector.bn_aggr(mv[:, r, :], stats[:, r, :]).then_inc(stat_step, 1)

            def guess_of(k, r):
                base = STAT * k
                dve.wait_ge(stat_step, base + 2)
                nc.vector.tensor_scalar(vare[:, r, :], mv[:, r, 1:2], LN_EPS, None, ALU.add).then_inc(stat_step, 1)
                dve.wait_ge(stat_step, base + 3)
                nc.vector.tensor_scalar(half_bits[:, r, :], vare[:, r, :].bitcast(INT32), 1, None,
                                        ALU.logical_shift_right).then_inc(stat_step, 1)
                dve.wait_ge(stat_step, base + 4)
                nc.vector.tensor_scalar(rs[0][:, r, :].bitcast(INT32), half_bits[:, r, :], -1.0, float(MAGIC),
                                        ALU.mult, ALU.add).then_inc(stat_step, 1)

            def stats_of(k, r):
                stats_waits(k)
                stats_first(k, r)
                stats_second_waits(k)
                stats_second(k, r)
                guess_of(k, r)

            def normalize(k, r):
                dve.wait_ge(newton, NEWTON * (k + 1))
                if past(k, 2):
                    dve.wait_ge(grad_done, k - 1)
                nc.vector.tensor_scalar(xn[:, r, :], x_all[:, k, :], mv[:, r, 0:1], rs[3][:, r, :],
                                        ALU.subtract, ALU.mult).then_inc(xn_ready, 1)

            steps = [0]

            def link(ins):
                steps[0] += 1
                ins.then_inc(setup_step, 1)
                dve.wait_ge(setup_step, steps[0])

            def scales_of(first, last):
                dve.wait_ge(all_ready, last // 2)
                c = slice(first, last)
                link(nc.vector.tensor_scalar(clamped[:, c], squares_all[:, c], 2.0 ** -40, None, ALU.max))
                link(nc.vector.tensor_scalar(halved[:, c], clamped[:, c].bitcast(INT32), 1, None,
                                             ALU.logical_shift_right))
                link(nc.vector.tensor_scalar(shifted[:, c], halved[:, c], float(129 << 22), None, ALU.add))
                link(nc.vector.tensor_scalar(power[:, c].bitcast(INT32), shifted[:, c], EXPONENT, None,
                                             ALU.bitwise_and))
                link(nc.vector.reciprocal(rpower[:, c], power[:, c]))
                link(nc.vector.tensor_scalar(unscale[:, c], power[:, c], 1.0 / (W_TOP * X_SCALE), None, ALU.mult))
                nc.vector.tensor_scalar(scale[:, c], rpower[:, c], W_TOP, None, ALU.mult).then_inc(scale_ready, 1)

            def lot_low(n):
                lot = slice(n * LOT, (n + 1) * LOT)
                dve.wait_ge(hi_ready, 3 + n)
                nc.vector.scalar_tensor_tensor(
                    out=w_lo[:, :, lot, :].rearrange("p h e d -> p h (e d)"),
                    in0=w_raw[:, :, lot, :].rearrange("p h e d -> p h (e d)"), scalar=scale[:, 2 + n:3 + n],
                    in1=w_hi[:, :, lot, :].rearrange("p h e d -> p h (e d)"), op0=ALU.mult,
                    op1=ALU.subtract).then_inc(lo_ready, 1)

            def low_parts(k, r):
                dve.wait_ge(xh_ready, k + 1)
                if past(k, 1):
                    dve.wait_ge(group_done[EXPERT_BANKS - 1], 2 * (k - 1)) if past(k, 2) else None
                dve.wait_ge(xt_ready, k + 1)
                nc.vector.scalar_tensor_tensor(out=xt_lo[:, r, :, :], in0=t_bank[:, :, 0:P], scalar=X_SCALE,
                                               in1=xt_hi[:, r, :, :], op0=ALU.mult,
                                               op1=ALU.subtract).then_inc(xl_ready, 1)

            def gram_out(k):
                dve.wait_ge(gram_done, k + 1)
                nc.vector.tensor_tensor(n1[:], inv_bank[:, 0, :], lower[:], ALU.mult)
                nc.vector.tensor_tensor(n1t[:], inv_bank[:, 0, :], upper[:], ALU.mult).then_inc(n1_ready, 1)

            def first_factor(k):
                dve.wait_ge(n1_ready, k + 1)
                if past(k, 1):
                    dve.wait_ge(s0_low, k)
                nc.vector.tensor_tensor(s0[:], ident[:], n1t[:], ALU.subtract).then_inc(first_ready, 1)

            def logits_out(k, r):
                dve.wait_ge(vr_done, k + 1)
                nc.vector.scalar_tensor_tensor(out=logit[:, r, :], in0=vr_bank[:, D:VR], scalar=unscale[:, 1:2],
                                               in1=rb_row[:], op0=ALU.mult, op1=ALU.add).then_inc(route, 1)
                if past(k, 2):
                    dve.wait_ge(y_ready, k - 1)
                nc.vector.tensor_tensor(v[:, r, :], vr_bank[:, 0:D], b_row[:], ALU.add).then_inc(v_ready, 1)

            def top_logit_waits(k):
                dve.wait_ge(route, ROUTE * k + 1)

            def top_logit(k, r):
                base = ROUTE * k
                nc.vector.max(top_l[:, r, :], logit[:, r, :]).then_inc(route, 1)
                dve.wait_ge(route, base + 2)
                nc.vector.tensor_scalar(neg_max[:, r, :], top_l[:, r, 0:1], -1.0, None, ALU.mult).then_inc(route, 1)

            def top_gates(k, r):
                base = ROUTE * k
                nc.vector.max(top_e[:, r, :], ex[:, r, 0:EXPERTS]).then_inc(route, 1)
                dve.wait_ge(route, base + 4)
                nc.vector.memset(top_e[:, r, TOP_K:8], -1.0).then_inc(route, 1)
                dve.wait_ge(route, base + 5)
                nc.vector.tensor_scalar(ex_eps[:, r, :], ex_sum[:, r, :], EPS, None, ALU.mult).then_inc(route, 1)
                nc.vector.match_replace(rest[:, r, :], top_e[:, r, :], ex[:, r, :], 0.0).then_inc(route, 1)
                dve.wait_ge(route, base + 7)
                nc.vector.scalar_tensor_tensor(out=sel[:, r, :], in0=ex[:, r, 0:EXPERTS], scalar=1.0,
                                               in1=rest[:, r, 0:EXPERTS], op0=ALU.mult, op1=ALU.subtract,
                                               accum_out=sel_sum[:, r, :]).then_inc(route, 1)

            def gates_norm(k, r):
                base = ROUTE * k
                dve.wait_ge(route, base + 8)
                nc.vector.tensor_tensor(denom[:, r, :], ex_eps[:, r, :], sel_sum[:, r, :], ALU.add).then_inc(route, 1)
                dve.wait_ge(route, base + 9)
                nc.vector.reciprocal(rdenom[:, r, :], denom[:, r, :]).then_inc(route, 1)
                dve.wait_ge(route, base + 10)
                nc.vector.tensor_scalar(acc[:, r, :], sel_sum[:, r, :], rdenom[:, r, :], EPS, ALU.mult,
                                        ALU.max).then_inc(route, 1)
                nc.vector.tensor_scalar(eps_term[:, r, :], sel_sum[:, r, :], rdenom[:, r, :], EPS, ALU.mult,
                                        ALU.mult).then_inc(route, 1)

            def gates_scaled(k, r):
                base = ROUTE * k
                dve.wait_ge(route, base + 11)
                nc.vector.reciprocal(racc[:, r, :], acc[:, r, :]).then_inc(route, 1)
                dve.wait_ge(route, base + 13)
                nc.vector.tensor_tensor(factor[:, r, :], rdenom[:, r, :], racc[:, r, :], ALU.mult).then_inc(route, 1)
                dve.wait_ge(route, base + 14)
                if past(k, 2):
                    dve.wait_ge(part_step, PS * (k - 1))
                if past(k, 1):
                    nc.vector.scalar_tensor_tensor(out=gate[:, r, :], in0=sel[:, r, :], scalar=factor[:, r, :],
                                                   in1=un_e[:], op0=ALU.mult, op1=ALU.mult).then_inc(route, 1)
                else:
                    nc.vector.tensor_scalar(gate[:, r, :], sel[:, r, :], factor[:, r, :], None,
                                            ALU.mult).then_inc(route, 1)

            def first_gates():
                link(nc.vector.tensor_copy(un_e[:].rearrange("p (n e) -> p n e", e=LOT),
                                           unscale[:, 2:2 + W_LOTS].unsqueeze(2).broadcast_to([P, W_LOTS, LOT])))
                nc.vector.tensor_tensor(gate[:, 0, :], gate[:, 0, :], un_e[:], ALU.mult).then_inc(first_gates_ready, 1)

            def second_factor(k):
                dve.wait_ge(p4_done, k + 1)
                dve.wait_ge(n4_ready, k + 1)
                nc.vector.tensor_tensor(s0[0:P - TWO, TWO:P], s0[0:P - TWO, TWO:P], inv_bank[0:P - TWO, 2, TWO:P],
                                        ALU.add).then_inc(s2_ready, 1)

            def third_factor(k):
                dve.wait_ge(prod4_done, k + 1)
                nc.vector.tensor_tensor(s0[0:P - FOUR, FOUR:P], s0[0:P - FOUR, FOUR:P], inv_bank[0:P - FOUR, 1, FOUR:P],
                                        ALU.add).then_inc(s4_ready, 1)

            def fourth_factor(k):
                dve.wait_ge(s0_done, k + 1)
                nc.vector.tensor_tensor(s0[0:P - EIGHT, EIGHT:P], s0[0:P - EIGHT, EIGHT:P], inv_bank[0:P - EIGHT, 2, EIGHT:P],
                                        ALU.add).then_inc(s0_ready, 1)

            def residual(k):
                dve.wait_ge(mem_done, k + 1)
                nc.vector.tensor_tensor(resid[:], mem_bank[:, 0:D], b_row[:], ALU.subtract).then_inc(resid_ready, 1)

            def low_residual(k):
                dve.wait_ge(resid_high, k + 1)
                nc.vector.tensor_tensor(resid_lo[:], resid[:], resid_hi[:].bitcast(FP32),
                                        ALU.subtract).then_inc(resid_low, 1)

            def low_err(k, r):
                dve.wait_ge(err_high, k + 1)
                if past(k, 1):
                    dve.wait_ge(grad_done, k)
                nc.vector.tensor_tensor(err_lo[:], err[:, r, :], err_hi[:].bitcast(FP32),
                                        ALU.subtract).then_inc(err_low, 1)

            def low_state(k):
                dve.wait_ge(state_high, k + 1)
                nc.vector.tensor_tensor(state_lo[:], state[:], state_hi[:].bitcast(FP32),
                                        ALU.subtract).then_inc(state_low, 1)

            def update(k):
                dve.wait_ge(grad_done, k + 1)
                flat = state[:].rearrange("p h e -> p (h e)")
                nc.vector.scalar_tensor_tensor(out=flat, in0=mem_bank[:], scalar=neg_c[:], in1=flat,
                                               op0=ALU.mult, op1=ALU.add).then_inc(state_ready, 1)

            def group(k, r, n):
                g = DVE_GROUPS[n]
                bank = g % EXPERT_BANKS
                base = ZS * k
                dve.wait_ge(group_done[bank], 2 * k + (g // EXPERT_BANKS + 1))
                if n == 0:
                    dve.wait_ge(route, ROUTE * (k + 1))
                    if not past(k, 1):
                        dve.wait_ge(first_gates_ready, 1)
                    if past(k, 2):
                        dve.wait_ge(z_sum, 2 * (k - 1))
                for j in range(2):
                    e = 2 * g + j
                    src = e_bank[bank][:, j * D:(j + 1) * D]
                    if n == 0:
                        nc.vector.tensor_scalar(zacc[:, r, j, :], src, gate[:, r, e:e + 1],
                                                None if j else eps_term[:, r, :], ALU.mult,
                                                ALU.bypass if j else ALU.add).then_inc(z_step, 1)
                    else:
                        dve.wait_ge(z_step, base + (2 * n + j - 1))
                        nc.vector.scalar_tensor_tensor(out=zacc[:, r, j, :], in0=src, scalar=gate[:, r, e:e + 1],
                                                       in1=zacc[:, r, j, :], op0=ALU.mult,
                                                       op1=ALU.add).then_inc(z_step, 1)

            def gated(k, r):
                dve.wait_ge(silu_ready, k + 1)
                dve.wait_ge(y_ready, k + 1)
                if past(k, 2):
                    dve.wait_ge(out_ready, k - 1)
                nc.vector.scalar_tensor_tensor(out=sg[:, r, :], in0=silu2[:, r, :], scalar=half_unq[:],
                                               in1=y[:, r, :], op0=ALU.mult, op1=ALU.mult).then_inc(sg_ready, 1)

            for k in range(2):
                stats_of(k, k)
            dve.wait_ge(small_loaded, 64)
            link(nc.vector.tensor_scalar(neg_c[:], eta[:], -2.0 / (BATCH * D), None, ALU.mult))
            dve.wait_ge(const_ready, 3)
            link(nc.vector.tensor_scalar(c_pos[:], neg_c[:], -1.0 / X_SCALE ** 2, None, ALU.mult))
            scales_of(0, 2)
            normalize(0, 0)
            dve.wait_ge(scale_ready, 1)
            link(nc.vector.tensor_scalar(q[:], scale[:, 0:1], X_SCALE, None, ALU.mult))
            nc.vector.tensor_scalar(half_unq[:], unscale[:, 0:1], 0.5, None, ALU.mult)
            nc.vector.tensor_scalar(lower[:], lower[:], c_pos[:], None, ALU.mult).then_inc(mask_scaled, 1)
            nc.vector.tensor_scalar(upper[:], upper[:], c_pos[:], None, ALU.mult).then_inc(mask_scaled, 1)
            for n, c in ((0, slice(0, D)), (1, slice(D, VR))):
                dve.wait_ge(hi_ready, n + 1)
                nc.vector.scalar_tensor_tensor(out=vr_lo[:, :, c], in0=vr_raw[:, :, c], scalar=scale[:, n:n + 1],
                                               in1=vr_hi[:, :, c], op0=ALU.mult, op1=ALU.subtract).then_inc(lo_ready, 1)

            low_parts(0, 0)
            nc.vector.tensor_scalar(b_row[:], b_row[:], q[:], None, ALU.mult).then_inc(setup_step, 1)
            steps[0] += 1
            b_scaled = steps[0]
            dve.wait_ge(mask_scaled, 2)
            gram_out(0)
            first_factor(0)
            link(nc.vector.tensor_tensor(state[:], state[:], vr_raw[:, :, 0:D], ALU.subtract))
            scales_of(2, 4)
            dve.wait_ge(setup_step, b_scaled)
            logits_out(0, 0)
            top_logit_waits(0)
            link(nc.vector.tensor_scalar(state[:], state[:], q[:], None, ALU.mult))
            top_logit(0, 0)
            second_factor(0)
            nc.vector.tensor_copy(state_hi[:], state[:]).then_inc(state_high, 1)
            normalize(1, 1)
            stats_waits(2)
            stats_first(2, 0)
            stats_second_waits(2)
            third_factor(0)
            stats_second(2, 0)
            low_state(0)
            guess_of(2, 0)
            lot_low(0)
            scales_of(4, 6)

            def body(k, r):
                nxt, nn, nnn = exists(k + 1), exists(k + 2), exists(k + 3)
                if nxt:
                    low_parts(k + 1, 1 - r)
                fourth_factor(k)
                residual(k)
                if past(k, 1):
                    gates_scaled(k, r)
                else:
                    lot_low(1)
                low_residual(k)
                if past(k, 1):
                    group(k, r, 0)
                    if nnn:
                        stats_waits(k + 3)
                    if nxt:
                        gram_out(k + 1)
                        logits_out(k + 1, 1 - r)
                        first_factor(k + 1)
                        top_logit_waits(k + 1)
                    low_err(k, r)
                    if nxt:
                        top_logit(k + 1, 1 - r)
                else:
                    gram_out(k + 1)
                    first_factor(k + 1)
                    scales_of(6, 10)
                    lot_low(2)
                    low_err(k, r)
                    dve.wait_ge(ex_ready, 1)
                    lot_low(3)
                    top_gates(k, r)
                    gates_norm(k, r)
                    gates_scaled(k, r)
                    first_gates()
                    group(k, r, 0)
                    logits_out(k + 1, 1 - r)
                    top_logit_waits(k + 1)
                    stats_waits(k + 3)
                    top_logit(k + 1, 1 - r)
                if nnn:
                    stats_first(k + 3, 1 - r)
                    stats_second_waits(k + 3)
                group(k, r, 1)
                if nnn:
                    stats_second(k + 3, 1 - r)
                update(k)
                if nnn:
                    guess_of(k + 3, 1 - r)
                if past(k, 1):
                    gated(k - 1, 1 - r)
                else:
                    lot_low(6)
                low_state(k + 1)
                if nxt:
                    second_factor(k + 1)
                    dve.wait_ge(ex_ready, k + 2)
                group(k, r, 2)
                if nn:
                    normalize(k + 2, r)
                group(k, r, 3)
                if nxt:
                    top_gates(k + 1, 1 - r)
                    third_factor(k + 1)
                    gates_norm(k + 1, 1 - r)
                group(k, r, 4)
                group(k, r, 5)

            in_loop(dve, body)

            k, r = CHUNKS - 1, (CHUNKS - 1) % 2
            dve.wait_ge(z_step, ZS * (k + 1))
            dve.wait_ge(z_sum, 2 * k)
            nc.vector.tensor_tensor(zeo[:], zacc[:, r, 0, :], zacc[:, r, 1, :], ALU.add).then_inc(z_sum, 1)
            dve.wait_ge(part_sum, 3 * (k + 1))
            dve.wait_ge(z_sum, 2 * k + 1)
            nc.vector.tensor_tensor(z[:, r, :], zeo[:], parts[:], ALU.add).then_inc(z_sum, 1)
            dve.wait_ge(th_ready, k + 1)
            dve.wait_ge(z_sum, 2 * k + 2)
            nc.vector.scalar_tensor_tensor(out=silu2[:, r, :], in0=th[:, r, :], scalar=1.0, in1=z[:, r, :],
                                           op0=ALU.add, op1=ALU.mult).then_inc(silu_ready, 1)
            gated(k, r)
            dve.wait_ge(sg_ready, k + 1)
            dve.wait_ge(out_ready, k)
            nc.vector.tensor_tensor(x_all[:, k, :], sg[:, r, :], x_all[:, k, :], ALU.add).then_inc(out_ready, 1)

        @block.tensor
        def _(pe):
            def transposes(k, r):
                pe.wait_ge(xn_ready, k + 1)
                if past(k, 1):
                    pe.wait_ge(xl_ready, k)
                for h in range(HALVES):
                    last = nc.tensor.transpose(t_bank[:, h, 0:P], xn[:, r, h * P:(h + 1) * P], ident[:])
                last.then_inc(transposed, 1)

            def split_product(dst, r, hi, lo):
                for h in range(HALVES):
                    nc.tensor.matmul(dst, xt_hi[:, r, h, :], hi(h), start=(h == 0), stop=False)
                    nc.tensor.matmul(dst, xt_hi[:, r, h, :], lo(h), start=False, stop=False)
                for h in range(HALVES):
                    last = nc.tensor.matmul(dst, xt_lo[:, r, h, :], hi(h), start=False, stop=(h == HALVES - 1))
                return last

            def values_and_gram(k, r):
                pe.wait_ge(xh_ready, k + 1)
                pe.wait_ge(xl_ready, k + 1)
                if past(k, 1):
                    pe.wait_ge(v_ready, k)
                    pe.wait_ge(s0_ready, k)
                values, square = vr_bank[:, 0:VR], inv_bank[:, 0, :]
                hi, lo = xt_hi[:, r], xt_lo[:, r]
                for h in range(HALVES):
                    nc.tensor.matmul(values, hi[:, h, :], vr_hi[:, h, :], start=(h == 0), stop=False)
                    nc.tensor.matmul(square, hi[:, h, :], hi[:, h, :], start=(h == 0), stop=False)
                    nc.tensor.matmul(values, hi[:, h, :], vr_lo[:, h, :], start=False, stop=False)
                    nc.tensor.matmul(square, hi[:, h, :], lo[:, h, :], start=False, stop=False)
                for h in range(HALVES):
                    last_value = nc.tensor.matmul(values, lo[:, h, :], vr_hi[:, h, :], start=False, stop=(h == HALVES - 1))
                    last = nc.tensor.matmul(square, lo[:, h, :], hi[:, h, :], start=False, stop=(h == HALVES - 1))
                last_value.then_inc(vr_done, 1)
                last.then_inc(gram_done, 1)

            def squares(k):
                pe.wait_ge(n1_ready, k + 1)
                nc.tensor.matmul(inv_bank[:, 0, 0:P - TWO], n1t[:], n1[:, 0:P - TWO], start=True, stop=True)
                nc.tensor.matmul(inv_bank[:, 1, TWO:P], n1[:], n1t[:, TWO:P], start=True, stop=True).then_inc(p2_done, 1)

            def fourths(k):
                pe.wait_ge(n2_ready, k + 1)
                pe.wait_ge(first_ready, k + 1)
                nc.tensor.matmul(inv_bank[:, 0, 0:P - FOUR], n2t[:], n2[:, 0:P - FOUR], start=True, stop=True)
                nc.tensor.matmul(inv_bank[0:P - TWO, 2, TWO:P], n2[:, 0:P - TWO], s0[:, TWO:P], start=True,
                                 stop=True).then_inc(p4_done, 1)

            def product4(k):
                pe.wait_ge(n4_ready, k + 1)
                pe.wait_ge(s2_ready, k + 1)
                nc.tensor.matmul(inv_bank[0:P - FOUR, 1, FOUR:P], n4[:, 0:P - FOUR], s0[:, FOUR:P], start=True,
                                 stop=True).then_inc(prod4_done, 1)

            def half_of_8(k):
                pe.wait_ge(s4_ready, k + 1)
                nc.tensor.matmul(inv_bank[0:P - FOUR, 3, EIGHT:P], n4[:, 0:P - FOUR], s0[:, EIGHT:P], start=True,
                                 stop=True).then_inc(half8_done, 1)

            def product8(k):
                pe.wait_ge(half8_ready, k + 1)
                nc.tensor.matmul(inv_bank[0:P - EIGHT, 2, EIGHT:P], n4[:, 0:P - EIGHT], half8[:, EIGHT:P], start=True,
                                 stop=True).then_inc(s0_done, 1)

            def memory(k):
                pe.wait_ge(xr_high, k + 1)
                pe.wait_ge(xr_low, k + 1)
                pe.wait_ge(state_high, k + 1)
                pe.wait_ge(state_low, k + 1)
                if past(k, 1):
                    pe.wait_ge(state_ready, k)
                dst = mem_bank[:, 0:D]
                for h in range(HALVES):
                    nc.tensor.matmul(dst, xr_hi[:, h, :], state_hi[:, h, :], start=(h == 0), stop=False)
                    nc.tensor.matmul(dst, xr_hi[:, h, :], state_lo[:, h, :], start=False, stop=False)
                    last = nc.tensor.matmul(dst, xr_lo[:, h, :], state_hi[:, h, :], start=False,
                                            stop=(h == HALVES - 1))
                last.then_inc(mem_done, 1)

            def errors(k):
                pe.wait_ge(s0_high, k + 1)
                pe.wait_ge(s0_low, k + 1)
                pe.wait_ge(resid_high, k + 1)
                pe.wait_ge(resid_low, k + 1)
                dst = mem_bank[:, D:2 * D]
                nc.tensor.matmul(dst, s0_hi[:], resid_hi[:], start=True, stop=False)
                nc.tensor.matmul(dst, s0_hi[:], resid_lo[:], start=False, stop=False)
                nc.tensor.matmul(dst, s0_lo[:], resid_hi[:], start=False, stop=True).then_inc(err_done, 1)

            def gradient(k):
                pe.wait_ge(rows_high, k + 1)
                pe.wait_ge(rows_low, k + 1)
                pe.wait_ge(err_high, k + 1)
                pe.wait_ge(err_low, k + 1)
                for h in range(HALVES):
                    dst, rows = mem_bank[:, h * D:(h + 1) * D], slice(h * P, (h + 1) * P)
                    nc.tensor.matmul(dst, xn_hi[:, rows], err_hi[:], start=True, stop=False)
                    nc.tensor.matmul(dst, xn_hi[:, rows], err_lo[:], start=False, stop=False)
                    last = nc.tensor.matmul(dst, xn_lo[:, rows], err_hi[:], start=False, stop=True)
                last.then_inc(grad_done, 1)

            def experts(k, r, g):
                bank = g % EXPERT_BANKS
                if isinstance(k, int) and k == 0 and g < EXPERT_BANKS:
                    pass
                elif (g - EXPERT_BANKS) % GROUPS in ACT_GROUPS:
                    n = ACT_GROUPS.index((g - EXPERT_BANKS) % GROUPS)
                    pe.wait_ge(part_step, PS * (k if g >= EXPERT_BANKS else k - 1) + 2 * (n + 1))
                else:
                    n = DVE_GROUPS.index((g - EXPERT_BANKS) % GROUPS)
                    pe.wait_ge(z_step, ZS * (k if g >= EXPERT_BANKS else k - 1) + 2 * (n + 1))
                if isinstance(k, int) and k == 0:
                    pe.wait_ge(hi_ready, 3 + 2 * g // LOT)
                    if 2 * g // LOT in POOL_LOTS:
                        pe.wait_ge(pool_low_ready, POOL_LOTS.index(2 * g // LOT) + 1)
                    else:
                        pe.wait_ge(lo_ready, 3 + DVE_LOTS.index(2 * g // LOT))
                split_product(e_bank[bank][:], r, lambda h: w_hi[:, h, 2 * g:2 * g + 2, :],
                              lambda h: w_lo[:, h, 2 * g:2 * g + 2, :]).then_inc(group_done[bank], 1)

            pe.wait_ge(const_ready, 1)
            transposes(0, 0)
            pe.wait_ge(hi_ready, 2)
            pe.wait_ge(lo_ready, 2)
            values_and_gram(0, 0)
            squares(0)
            fourths(0)
            product4(0)
            half_of_8(0)

            def body(k, r):
                more = exists(k + 1)
                if more:
                    transposes(k + 1, 1 - r)
                memory(k)
                product8(k)
                experts(k, r, 0)
                if more:
                    values_and_gram(k + 1, 1 - r)
                experts(k, r, 1)
                errors(k)
                if more:
                    squares(k + 1)
                experts(k, r, 2)
                gradient(k)
                experts(k, r, 3)
                if more:
                    fourths(k + 1)
                experts(k, r, 4)
                experts(k, r, 5)
                if more:
                    product4(k + 1)
                experts(k, r, 6)
                experts(k, r, 7)
                if more:
                    half_of_8(k + 1)

            in_loop(pe, body)


def kernel(L0_attn_x, L0_attn_W0, L0_attn_Wkv, L0_attn_bkv, L0_attn_eta, L0_ffn_router_w, L0_ffn_router_b,
           L0_ffn_expert_w):
    import numpy as np
    import concourse.bacc as bacc
    from concourse.bass_utils import run_bass_kernel_spmd

    def halves(w):
        return np.ascontiguousarray(np.asarray(w).reshape(HALVES, P, -1).transpose(1, 0, 2))

    x = np.asarray(L0_attn_x)
    wkv, bkv = np.asarray(L0_attn_Wkv), np.asarray(L0_attn_bkv)
    rows = x.transpose(1, 0, 2).reshape(CHUNKS, P, D).transpose(1, 0, 2)
    arrays = {
        "x_rows": np.ascontiguousarray(rows),
        "w0_t": halves(np.asarray(L0_attn_W0).T),
        "wv_router_t": halves(np.concatenate([wkv[D:].T, np.asarray(L0_ffn_router_w).T], axis=1)),
        "experts": np.ascontiguousarray(
            np.asarray(L0_ffn_expert_w).reshape(EXPERTS, HALVES, P, D).transpose(2, 1, 0, 3)),
        "bias_v": np.ascontiguousarray(bkv[D:].reshape(1, D)),
        "router_b": np.ascontiguousarray(np.asarray(L0_ffn_router_b).reshape(1, EXPERTS)),
        "eta_in": np.ascontiguousarray(np.asarray(L0_attn_eta).reshape(1, 1)),
    }
    nc = bacc.Bacc("TRN2", target_bir_lowering=False, num_devices=1)
    args = [nc.dram_tensor(n, a.shape, mybir.dt.from_np(a.dtype), kind="ExternalInput").ap()
            for n, a in arrays.items()]
    out = nc.dram_tensor("out_rows", (P, CHUNKS, D), FP32, kind="ExternalOutput").ap()
    program(nc, *args, out)
    result = run_bass_kernel_spmd(nc, [arrays], core_ids=[0])
    got = np.asarray(result.results[0]["out_rows"])
    return np.ascontiguousarray(got.transpose(1, 0, 2).reshape(STEPS, BATCH, D).transpose(1, 0, 2))
```
